# Optimizing a Trainium2 kernel written in Bass

```python
import numpy as np
import jax
import jax.numpy as jnp

def _softmax(x, axis=-1):
    return jax.nn.softmax(x, axis=axis)

def _gelu(x):
    return jax.nn.gelu(x, approximate=True)

def _silu(x):
    return jax.nn.silu(x)

def _sigmoid(x):
    return jax.nn.sigmoid(x)

def _layernorm(x, axis=-1, eps=1e-05):
    m = jnp.mean(x, axis=axis, keepdims=True)
    v = jnp.var(x, axis=axis, keepdims=True)
    return (x - m) / jnp.sqrt(v + eps)

def _scatter_add(tgt, idx, src, axis=0):
    return tgt.at[idx].add(src)

def _segment_sum(src, seg, n):
    return jax.ops.segment_sum(src, seg, n)
kernel_name = 'mk_decoder_postln_d1_seqx_r8_e7f242'

def setup_inputs(seed: int=0):
    np.random.seed(seed)
    _w = jnp.asarray

    def _rec_inputs():
        import jax
        import jax.numpy as jnp
        _rk = jax.random.key(seed)
        x = 7.22e-05 + 1 * jax.random.normal(jax.random.fold_in(_rk, 1), (32, 128, 128), jnp.float32)
        _lenS = 128 - jax.random.randint(jax.random.fold_in(_rk, 7), (32,), 0, max(1, 128 // 4) + 1, jnp.int32)
        _lenS2 = 77 - jax.random.randint(jax.random.fold_in(_rk, 8), (32,), 0, max(1, 77 // 4) + 1, jnp.int32)
        _ctx_1024P = jax.random.normal(jax.random.fold_in(_rk, 11), (32, 16, 128), jnp.float32)
        _ctx_1024c = jax.random.dirichlet(jax.random.fold_in(_rk, 511), 0.3 * jnp.ones((16,), jnp.float32), (32, 77))
        _ctx_1024t = jnp.einsum('bsk,bkd->bsd', _ctx_1024c, _ctx_1024P)
        _ctx_1024t = _ctx_1024t * jax.lax.rsqrt(jnp.mean(jnp.square(_ctx_1024t)) + 1e-12) * 0.953939
        ctx_1024 = 4.13588e-05 + 0.999923 * (_ctx_1024t + 0.3 * jax.random.normal(jax.random.fold_in(_rk, 611), (32, 77, 128), jnp.float32))
        return (x, ctx_1024)
    x, ctx_1024 = _rec_inputs()

    def _L0_attn_setup():
        import jax, jax.numpy as jnp
        import numpy as np
        HIDDEN = 128
        D_COMPLEX = HIDDEN // 2
        key = jax.random.key(seed)
        ks = jax.random.split(key, 9)
        B, S, H = (4, 512, HIDDEN)
        scale = 1.0 / np.sqrt(H)
        inp = {'x': jax.random.normal(ks[0], (B, S, H), dtype=jnp.float32), 'Wq': jax.random.normal(ks[1], (H, H), dtype=jnp.float32) * scale, 'bq': jnp.zeros((H,), dtype=jnp.float32), 'Wk': jax.random.normal(ks[2], (H, H), dtype=jnp.float32) * scale, 'bk': jnp.zeros((H,), dtype=jnp.float32), 'Wv': jax.random.normal(ks[3], (H, H), dtype=jnp.float32) * scale, 'bv': jnp.zeros((H,), dtype=jnp.float32), 'Wo': jax.random.normal(ks[4], (H, H), dtype=jnp.float32) * scale, 'bo': jnp.zeros((H,), dtype=jnp.float32)}
        return inp
    _L0_attn_all = _L0_attn_setup()
    _L0_attn_in = {k: v for k, v in _L0_attn_all.items() if k in ('Wq', 'bq', 'Wk', 'bk', 'Wv', 'bv', 'Wo', 'bo')}
    del _L0_attn_all

    def _L0_xattn_setup():
        import jax, jax.numpy as jnp
        import numpy as np
        H, D_MODEL, D_K, D_V = (16, 128, 64, 64)
        B, S = (4, 256)

        def _xavier(key, shape):
            fan_in, fan_out = (shape[-2], shape[-1])
            limit = jnp.sqrt(6.0 / (fan_in + fan_out))
            return jax.random.uniform(key, shape, jnp.float32, -limit, limit)
        key = jax.random.key(seed)
        kq, kk, kv, kwq, kwk, kwv, kwo = jax.random.split(key, 7)
        return {'Q': jax.random.normal(kq, (B, S, D_MODEL), jnp.float32), 'K': jax.random.normal(kk, (B, S, D_MODEL), jnp.float32), 'V': jax.random.normal(kv, (B, S, D_MODEL), jnp.float32), 'W_Q': _xavier(kwq, (H, D_MODEL, D_K)), 'W_K': _xavier(kwk, (H, D_MODEL, D_K)), 'W_V': _xavier(kwv, (H, D_MODEL, D_V)), 'W_O': _xavier(kwo, (H * D_V, D_MODEL))}
    _L0_xattn_all = _L0_xattn_setup()
    _L0_xattn_in = {k: v for k, v in _L0_xattn_all.items() if k in ('W_Q', 'W_K', 'W_V', 'W_O')}
    del _L0_xattn_all

    def _L0_ffn_setup():
        import jax, jax.numpy as jnp
        import numpy as np
        from math import ceil
        CAPACITY_FACTOR = 2.0
        MIN_CAPACITY = 4
        key = jax.random.key(seed)
        ks = jax.random.split(key, 4)
        B, S, D, Di, E = (4, 256, 128, 512, 8)
        x = jax.random.normal(ks[0], (B, S, D), dtype=jnp.float32)
        Wr = jax.random.normal(ks[1], (D, E), dtype=jnp.float32) * D ** (-0.5)
        W1 = jax.random.normal(ks[2], (E, D, Di), dtype=jnp.float32) * D ** (-0.5)
        b1 = jnp.zeros((E, Di), dtype=jnp.float32)
        W2 = jax.random.normal(ks[3], (E, Di, D), dtype=jnp.float32) * Di ** (-0.5)
        b2 = jnp.zeros((E, D), dtype=jnp.float32)
        return {'x': x, 'Wr': Wr, 'W1': W1, 'b1': b1, 'W2': W2, 'b2': b2}
    _L0_ffn_all = _L0_ffn_setup()
    _L0_ffn_in = {k: v for k, v in _L0_ffn_all.items() if k in ('Wr', 'W1', 'b1', 'W2', 'b2')}
    del _L0_ffn_all
    return {'x': x, 'ctx_1024': ctx_1024, 'L0_attn_Wq': _L0_attn_in['Wq'], 'L0_attn_bq': _L0_attn_in['bq'], 'L0_attn_Wk': _L0_attn_in['Wk'], 'L0_attn_bk': _L0_attn_in['bk'], 'L0_attn_Wv': _L0_attn_in['Wv'], 'L0_attn_bv': _L0_attn_in['bv'], 'L0_attn_Wo': _L0_attn_in['Wo'], 'L0_attn_bo': _L0_attn_in['bo'], 'L0_xattn_W_Q': _L0_xattn_in['W_Q'], 'L0_xattn_W_K': _L0_xattn_in['W_K'], 'L0_xattn_W_V': _L0_xattn_in['W_V'], 'L0_xattn_W_O': _L0_xattn_in['W_O'], 'L0_ffn_Wr': _L0_ffn_in['Wr'], 'L0_ffn_W1': _L0_ffn_in['W1'], 'L0_ffn_b1': _L0_ffn_in['b1'], 'L0_ffn_W2': _L0_ffn_in['W2'], 'L0_ffn_b2': _L0_ffn_in['b2']}

def reference(x, ctx_1024, L0_attn_Wq, L0_attn_bq, L0_attn_Wk, L0_attn_bk, L0_attn_Wv, L0_attn_bv, L0_attn_Wo, L0_attn_bo, L0_xattn_W_Q, L0_xattn_W_K, L0_xattn_W_V, L0_xattn_W_O, L0_ffn_Wr, L0_ffn_W1, L0_ffn_b1, L0_ffn_W2, L0_ffn_b2):
    import jax
    import jax.numpy as jnp

    def _L0_attn_ref(x, Wq, bq, Wk, bk, Wv, bv, Wo, bo):
        import jax, jax.numpy as jnp
        import numpy as np
        HIDDEN = 128
        D_COMPLEX = HIDDEN // 2
        Q = x @ Wq.T + bq
        K = x @ Wk.T + bk
        V = x @ Wv.T + bv
        scores = jnp.einsum('bqd,bkd->bqk', Q, K) / np.sqrt(D_COMPLEX)
        weights = jax.nn.softmax(scores, axis=-1)
        out = jnp.einsum('bqk,bkd->bqd', weights, V)
        return out @ Wo.T + bo

    def _L0_xattn_ref(Q, K, V, W_Q, W_K, W_V, W_O):
        import jax, jax.numpy as jnp
        import numpy as np
        H, D_MODEL, D_K, D_V = (16, 128, 64, 64)
        B, S = (4, 256)

        def _xavier(key, shape):
            fan_in, fan_out = (shape[-2], shape[-1])
            limit = jnp.sqrt(6.0 / (fan_in + fan_out))
            return jax.random.uniform(key, shape, jnp.float32, -limit, limit)
        q = jnp.einsum('bsm,hmk->bhsk', Q, W_Q)
        k = jnp.einsum('bsm,hmk->bhsk', K, W_K)
        v = jnp.einsum('bsm,hmv->bhsv', V, W_V)
        scale = 1.0 / jnp.sqrt(jnp.asarray(q.shape[-1], q.dtype))
        scores = jnp.einsum('bhqk,bhsk->bhqs', q, k) * scale
        attn = jax.nn.softmax(scores, axis=-1)
        heads = jnp.einsum('bhqs,bhsv->bhqv', attn, v)
        concat = jnp.transpose(heads, (0, 2, 1, 3)).reshape(Q.shape[0], Q.shape[1], -1)
        return concat @ W_O

    def _L0_ffn_ref(x, Wr, W1, b1, W2, b2):
        import jax, jax.numpy as jnp
        import numpy as np
        from math import ceil
        CAPACITY_FACTOR = 2.0
        MIN_CAPACITY = 4
        B, S, D = x.shape
        E = Wr.shape[1]
        N = B * S
        k = max(MIN_CAPACITY, ceil(N * CAPACITY_FACTOR / E))
        xt = x.reshape(N, D)
        scores = jax.nn.softmax(xt @ Wr, axis=-1)
        G, idx = jax.lax.top_k(scores.T, k)
        X_in = xt[idx]
        h = jax.nn.gelu(jnp.einsum('ekd,edh->ekh', X_in, W1) + b1[:, None, :], approximate=False)
        X_e = jnp.einsum('ekh,ehd->ekd', h, W2) + b2[:, None, :]
        contrib = (G[..., None] * X_e).reshape(E * k, D)
        out = jnp.zeros((N, D), dtype=x.dtype).at[idx.reshape(-1)].add(contrib)
        return out.reshape(B, S, D)
    x = _layernorm(x + _L0_attn_ref(x, L0_attn_Wq, L0_attn_bq, L0_attn_Wk, L0_attn_bk, L0_attn_Wv, L0_attn_bv, L0_attn_Wo, L0_attn_bo), axis=-1)
    x = _layernorm(x + _L0_xattn_ref(x, ctx_1024, ctx_1024, L0_xattn_W_Q, L0_xattn_W_K, L0_xattn_W_V, L0_xattn_W_O), axis=-1)
    x = _layernorm(x + _L0_ffn_ref(x, L0_ffn_Wr, L0_ffn_W1, L0_ffn_b1, L0_ffn_W2, L0_ffn_b2), axis=-1)
    return x

_drawn_inputs = setup_inputs


def setup_inputs(seed=0):
    import zlib

    import numpy as np

    out = dict(_drawn_inputs(seed))
    spreads = {'L0_attn_bq': (0.0, 0.1),
     'L0_attn_bk': (0.0, 0.8),
     'L0_attn_bv': (0.0, 0.1),
     'L0_attn_bo': (0.0, 0.1),
     'L0_ffn_b1': (0.0, 0.287),
     'L0_ffn_b2': (0.0, 0.1)}
    factors = {}
    for name, (base, spread) in spreads.items():
        noise = np.random.default_rng([zlib.crc32(name.encode()), seed]).standard_normal(out[name].shape)
        drawn = base * np.exp(spread * noise) if base else spread * noise
        out[name] = jnp.asarray(drawn.astype(out[name].dtype))
    for name, factor in factors.items():
        out[name] = (out[name] * factor).astype(out[name].dtype)
    return out
```

```python
from contextlib import ExitStack

import concourse.bass as bass
from concourse import mybir

ALU = mybir.AluOpType
ACT = mybir.ActivationFunctionType
AX = mybir.AxisListType
F32 = mybir.dt.float32
BF16 = mybir.dt.bfloat16
I32 = mybir.dt.int32

P = 128
B = 32
PAIRS = B // 2
KEYS = 77
HEADS = 16
DK = 64
HK = HEADS * KEYS
CH = -(-HK // P)
HKP = CH * P
E = 8
F = 512
FC = F // P
EPS = 1e-5
SELF_SCALE = 1.0 / 8.0
CROSS_SCALE = 1.0 / 8.0
ROW = P + E

RING_BANKS = 4
UNITS = (
    [("xT", "prep"), ("cT", "prep"), ("x2T", "post"), ("QK", "prep"), ("LG", "post"), ("V", "prep")]
    + [(("A", u), "prep") for u in range(7)]
    + [(("P2T", 0, g), "cross") for g in range(3)]
    + [(("A", 7), "prep"), (("VOT", 0), "prep"), (("AV2", 0), "cross")]
    + [(("VOT", u), "prep") for u in range(1, 5)]
    + [(("P2T", 1, g), "cross") for g in range(3)]
    + [(("VOT", u), "prep") for u in range(5, 8)]
    + [(("AV2", 1), "cross")]
    + [(("VO", e, g), "prep") for e in range(2) for g in range(3)]
)
assert len(UNITS) % RING_BANKS == 0
SLOT = {name: k for k, (name, _) in enumerate(UNITS)}
LEAD = {"prep": 1, "cross": 0, "post": -1}
GROUPS = [(0, 4), (4, 8), (8, CH)]
TOKENS = B * P
TOPK = max(4, -(-2 * TOKENS // E))
SB = TOPK // P
NONE = float(TOKENS)
ROUNDS = 15


def clip(n, most):
    return max(0, min(n, most)) if isinstance(n, int) else n


def bank_of(name):
    return SLOT[name] % RING_BANKS


def fills_before(step, name):
    k = SLOT[name]
    total = 0
    for j, (_, stage) in enumerate(UNITS):
        if j % RING_BANKS == k % RING_BANKS:
            total = total + clip(step + LEAD[stage] + (1 if j < k else 0), PAIRS)
    return total


def wait(eng, sem, count):
    if isinstance(count, int) and count <= 0:
        return
    eng.wait_ge(sem, count)


def wait_apart(eng, sem, count, passed):
    wait(eng, sem, count)
    if not isinstance(count, int):
        eng.sem_inc(passed, 1)


def attention_steps(eng, step):
    def at(p, parity, nth):
        steady = not isinstance(p, int)
        step(p, parity, nth, steady or p + 1 < PAIRS, steady or 0 <= p < PAIRS, steady or p > 0)

    at(-1, 1, 0)
    at(0, 0, 0)
    with eng.Fori(0, (PAIRS - 4) // 2) as i:
        at(2 * i + 1, 1, i + 1)
        at(2 * i + 2, 0, i + 1)
    for p in range(PAIRS - 3, PAIRS + 1):
        at(p, p % 2, (p + 1) // 2)


def decoder_layer(nc, x, ctx_1024, Wq, bq, Wk, bk, Wv, bv, Wo, bo, W_Q, W_K, W_V, W_O, Wr, W1, b1, W2, b2, out):
    ctx = ExitStack()
    with ctx:
        def sb(name, shape, dt=F32):
            return ctx.enter_context(nc.sbuf_tensor(name, shape, dt))

        def sem(name):
            return ctx.enter_context(nc.semaphore(name))

        PS = ctx.enter_context(nc.psum_tensor("PS", [P, 8, 512], F32))
        ring = [PS[:, 3 + k, :] for k in range(RING_BANKS)]
        small = PS[:, 7, :]

        ident = sb("ident", [P, P])
        ones = sb("ones", [P, P])
        mhalf = sb("mhalf", [P, 2])
        wself = sb("wself", [P, 4, P])
        brow = sb("brow", [1, P + E * P])
        bcol = sb("bcol", [P, 3])
        bvb = sb("bvb", [P, P])
        shared1 = sb("shared1", [P, 3 * SB * ROW])
        wheads = shared1[:, 0:3 * HEADS * DK].rearrange("p (w n) -> p w n", w=3)
        xg = shared1[:, :].rearrange("p (b s n) -> p b s n", b=3, s=SB)
        won = sb("won", [P, HEADS // 2, P])
        wT = sb("wT", [P, 3, P])
        wvo = sb("wvo", [P, 3, P])
        wheadsT = sb("wheadsT", [P, 3, HEADS // 2, P])
        shared2 = sb("shared2", [P, 2 * HEADS, P])
        MT = shared2[:, 0:HEADS, :]
        NN = shared2[:, HEADS:2 * HEADS, :]
        fin = shared2
        wr = sb("wr", [P, E])
        b1n = sb("b1n", [E * FC, P])
        b1T = sb("b1T", [P, E * FC])
        b2b = sb("b2b", [P, E, P])
        w1 = sb("w1", [P, E, F])
        w2 = sb("w2", [P, E, FC, P])
        xin = [sb(f"xin{k}", [P, 2, P]) for k in range(2)]
        cin = [sb(f"cin{k}", [KEYS, 2, P]) for k in range(2)]
        xbo = sb("xbo", [P, 2, P])
        xT = sb("xT", [P, 2, P])
        cT = sb("cT", [P, 2 * KEYS])
        qT = sb("qT", [P, 2, P])
        kT = sb("kT", [P, 2, P])
        vs = sb("vs", [P, 2, P])
        smax = sb("smax", [P, 2])
        snb = sb("snb", [P, 2])
        pself = sb("pself", [P, 2, P])
        ssum = sb("ssum", [P, 2])
        srcp = sb("srcp", [P, 2])
        pselfT = sb("pselfT", [P, 2, P])
        r1 = sb("r1", [P, 2, P])
        st1 = sb("st1", [P, 2, 6])
        mv1 = sb("mv1", [P, 2, 2])
        ve1 = sb("ve1", [P, 2])
        rs1 = sb("rs1", [P, 2])
        x1 = [sb(f"x1_{k}", [P, 2, P]) for k in range(2)]
        x1T = sb("x1T", [P, 2, P])
        shared3 = sb("shared3", [P, 4 * HK])
        A = [shared3[:, k * 2 * HK:(k + 1) * 2 * HK].rearrange("p (e n) -> p e n", e=2)
             for k in range(2)]
        hid = shared3[:, 0:FC * TOPK].rearrange("p (c t) -> p c t", c=FC)
        VOT = sb("VOT", [P, 2, HKP])
        VO = sb("VO", [P, 2, CH, P])
        pc = sb("pc", [P, 2, HK])
        onehot = pc[:, :, :].rearrange("p e n -> p (e n)")[:, 0:B * P // 2].bitcast(BF16).rearrange(
            "p (b s) -> p b s", b=B)
        pn = sb("pn", [P, 2, HKP])
        ye = pn[:, :, :].rearrange("p e n -> p (e n)")[:, 0:2 * TOPK].rearrange("p (b s d) -> p b s d", b=2, s=SB)
        pT = sb("pT", [P, 2, HKP])
        xeT = pT[:, 0, 0:TOPK]
        cmax = sb("cmax", [P, 2, HEADS])
        csum = sb("csum", [P, 2, HEADS])
        crcp = sb("crcp", [P, 2, HEADS])
        r2 = sb("r2", [P, 2, P])
        st2 = sb("st2", [P, 2, 6])
        mv2 = sb("mv2", [P, 2, 2])
        ve2 = sb("ve2", [P, 2])
        rs2 = sb("rs2", [P, 2])
        x2 = [sb(f"x2_{k}", [P, 2, P]) for k in range(2)]
        x2T = sb("x2T", [P, 2, P])
        logits = sb("logits", [P, B, E])
        gates = sb("gates", [P, B, E])
        gmax = sb("gmax", [P, B])
        gsum = sb("gsum", [P, B])
        grcp = sb("grcp", [P, B])
        gatesT = sb("gatesT", [P, 2 * P])
        above = sb("above", [P, 3, 2 * P], BF16)
        count = sb("count", [P, 2, 3], BF16)
        group = sb("group", [P, P], BF16)
        groupf = sb("groupf", [P, P])
        passed = sb("passed", [P, 3])
        npassed = sb("npassed", [P, 1])
        bits = sb("bits", [P, 1], I32)
        thr = sb("thr", [P, 2], I32)
        three = sb("three", [P, 3], I32)
        pattern = sb("pattern", [P, ROUNDS, 3], I32)
        cand = sb("cand", [P, 2, 3], I32)
        thr8 = sb("thr8", [E, E])
        thrb = sb("thrb", [P, E])
        before = sb("before", [P, P], BF16)
        beforef = sb("beforef", [P, P])
        onesb = sb("onesb", [P, P], BF16)
        keep = sb("keep", [P, 2 * E, B])
        taken = sb("taken", [P, 2, E, B], BF16)
        totals = sb("totals", [P, 2 * E * B])
        slot = sb("slot", [P, 2, E, B])
        slot2 = sb("slot2", [P, 2, E, B])
        sloti = sb("sloti", [P, E, B], I32)
        slotlo = sb("slotlo", [P, E, B], I32)
        slothi = sb("slothi", [P, E, B], I32)
        iota = sb("iota", [P, P], I32)
        iotab = sb("iotab", [P, B], I32)
        iotap = sb("iotap", [P, 1], I32)
        pcol = sb("pcol", [P, 1])
        hot8 = sb("hot8", [P, B, SB], BF16)
        tokens = sb("tokens", [P, B, SB, 2], BF16)
        idx = sb("idx", [P, E, SB], I32)
        yb = VO[:, 0, 0:SB, :]
        stf = sb("stf", [P, B, 6])
        mvf = sb("mvf", [P, B, 2])
        vef = sb("vef", [P, B])
        rsf = sb("rsf", [P, B])

        w_in = sem("w_in")
        x_in = [sem(f"x_in{k}") for k in range(2)]
        c_in = [sem(f"c_in{k}") for k in range(2)]
        consts = sem("consts")
        setup_full = sem("setup_full")
        setup_dve = sem("setup_dve")
        setup_act = sem("setup_act")
        full = [sem(f"ring_full{k}") for k in range(RING_BANKS)]
        free = [sem(f"ring_free{k}") for k in range(RING_BANKS)]
        self_full = sem("self_full")
        self_free = sem("self_free")
        s2_full = sem("s2_full")
        s2_free = sem("s2_free")
        cmax_done = sem("cmax_done")
        cexp_done = sem("cexp_done")
        csum_done = sem("csum_done")
        crcp_done = sem("crcp_done")
        pn_done = sem("pn_done")
        smax_done = sem("smax_done")
        snb_done = sem("snb_done")
        sexp_done = sem("sexp_done")
        srcp_done = sem("srcp_done")
        xbo_done = sem("xbo_done")
        ln1_steps = sem("ln1_steps")
        ln2_steps = sem("ln2_steps")
        r2_done = sem("r2_done")
        var1 = sem("var1")
        rstd1 = sem("rstd1")
        var2 = sem("var2")
        rstd2 = sem("rstd2")
        x1_done = sem("x1_done")
        x2_done = sem("x2_done")
        stored = [sem(f"stored{k}") for k in range(2)]
        passed_dve = sem("passed_dve")
        passed_sp = sem("passed_sp")
        chain = sem("chain")
        attended = sem("attended")
        moe_in = sem("moe_in")
        g_sub = sem("g_sub")
        g_exp = sem("g_exp")
        gates_done = sem("gates_done")
        gates_stored = sem("gates_stored")
        gatesT_full = sem("gatesT_full")
        counted = sem("counted")
        summed = sem("summed")
        thr8_done = sem("thr8_done")
        thrb_full = sem("thrb_full")
        taken_done = sem("taken_done")
        prefix_full = sem("prefix_full")
        onehot_done = sem("onehot_done")
        tokens_done = sem("tokens_done")
        list_full = sem("list_full")
        idx_done = sem("idx_done")
        gathered = [[sem(f"gathered{b}_{h}") for h in range(SB)] for b in range(3)]
        xeT_full = sem("xeT_full")
        xeT_done = sem("xeT_done")
        hid_full = sem("hid_full")
        hid_done = sem("hid_done")
        ye_full = sem("ye_full")
        ye_added = sem("ye_added")
        ye_done = sem("ye_done")
        scattered = sem("scattered")
        fin_in = [sem(f"fin_in{c}") for c in range(B // 4)]
        fin_var = sem("fin_var")
        fin_rstd = sem("fin_rstd")
        fin_done = sem("fin_done")
        out_done = sem("out_done")
        table = nc.dram_tensor("table", [TOKENS, ROW], F32, kind="Internal").ap()
        total = nc.dram_tensor("total", [TOKENS, P], F32, kind="Internal").ap()

        x_pairs = x.rearrange("(q e) t d -> q t e d", e=2)
        c_pairs = ctx_1024.rearrange("(q e) s d -> q s e d", e=2)

        def ring_wait_free(eng, step, name):
            wait(eng, free[bank_of(name)], fills_before(step, name))

        def ring_wait_full(eng, step, name):
            wait(eng, full[bank_of(name)], fills_before(step, name) + 1)

        def ring_wait_copied(eng, step, name):
            wait(eng, free[bank_of(name)], fills_before(step, name) + 1)

        setup = []
        NLOAD = 12

        HID_BANKS = (5, 6, 0)
        CONSTS = 15 + 2 * (P // E) - 1 + 3
        W_UNITS = 6
        SETUP_UNITS = 2 + W_UNITS + 8 + 4

        def setup_target(k):
            if k == 0:
                return wT[:, :, :].rearrange("p a b -> p (a b)"), 3 * P
            if k == 1:
                return wvo[:, :, :].rearrange("p a b -> p (a b)"), 3 * P
            if k < 2 + W_UNITS:
                w, g = divmod(k - 2, 2)
                return wheadsT[:, w, 4 * g:4 * g + 4, :].rearrange("p a b -> p (a b)"), 4 * P
            if k >= 2 + W_UNITS + 8:
                j = k - 2 - W_UNITS - 8
                if j == 0:
                    return b1T[:, :], E * FC
                if j == 1:
                    return group[:, :], P
                return b2b[:, 4 * (j - 2):4 * (j - 2) + 4, :].rearrange("p a b -> p (a b)"), 4 * P
            m, g = divmod(k - 2 - W_UNITS, 4)
            dst = (MT, NN)[m]
            return dst[:, :, :].rearrange("p (b i a) d -> p b a i d", a=2, i=4)[:, g // 2, g % 2, :, :], 4 * P

        block = ctx.enter_context(nc.Block())

        @block.sync
        def _(sp):
            sp.dma_start(wself[:, 0, :], Wq).then_inc(w_in, 16)
            sp.dma_start(wself[:, 1, :], Wk).then_inc(w_in, 16)
            sp.dma_start(wself[:, 2, :], Wv).then_inc(w_in, 16)
            sp.dma_start(wself[:, 3, :], Wo).then_inc(w_in, 16)
            sp.dma_start(brow[:, 0:P], bo.rearrange("(a n) -> a n", a=1)).then_inc(w_in, 16)
            sp.dma_start(bcol[:, 0:1], bq.rearrange("(n a) -> n a", a=1)).then_inc(w_in, 16)
            sp.dma_start(bcol[:, 1:2], bk.rearrange("(n a) -> n a", a=1)).then_inc(w_in, 16)
            sp.dma_start(bcol[:, 2:3], bv.rearrange("(n a) -> n a", a=1)).then_inc(w_in, 16)
            for k, w in enumerate((W_Q, W_K, W_V)):
                sp.dma_start(wheads[:, k, :].rearrange("m (h k) -> m h k", h=HEADS),
                             w.rearrange("h m k -> m h k")).then_inc(w_in, 16)
            sp.dma_start(won[:, :, :], W_O.rearrange("(c p) o -> p c o", p=P)).then_inc(w_in, 16)
            sp.dma_start(xin[0][:, :, :], x_pairs[0]).then_inc(x_in[0], 16)
            sp.dma_start(cin[0][:, :, :], c_pairs[0]).then_inc(c_in[0], 16)
            sp.dma_start(wr[:, :], Wr).then_inc(w_in, 16)
            sp.dma_start(b1n[:, :], b1.rearrange("e (c f) -> (e c) f", f=P)).then_inc(w_in, 16)
            sp.dma_start(brow[:, P:P + E * P], b2.rearrange("(a e) d -> a (e d)", a=1)).then_inc(w_in, 16)
            sp.dma_start(w1[:, :, :], W1.rearrange("e d f -> d e f")).then_inc(moe_in, 16)
            sp.dma_start(w2[:, :, :, :].rearrange("p e c d -> p (e c) d"),
                         W2.rearrange("e (c p) d -> p (e c) d", p=P)).then_inc(moe_in, 16)

            def load(step, parity, q):
                if not (isinstance(q, int) and q < 2):
                    for name in ("xT", "cT"):
                        wait_apart(sp, full[bank_of(name)], fills_before(step - 1, name) + 1, passed_sp)
                    wait_apart(sp, xbo_done, step + 1, passed_sp)
                sp.dma_start(xin[parity][:, :, :], x_pairs[q]).then_inc(x_in[parity], 16)
                sp.dma_start(cin[parity][:, :, :], c_pairs[q]).then_inc(c_in[parity], 16)

            def store(q, parity):
                wait_apart(sp, x2_done, 2 * q + 2, passed_sp)
                rows = 2 * P
                tab = table.rearrange("(q e t) d -> q t e d", e=2, t=P)
                sm = total.rearrange("(q e t) d -> q t e d", e=2, t=P)
                sp.dma_start(tab[q, :, :, 0:P], x2[parity][:, :, :]).then_inc(stored[parity], 16)
                sp.dma_start(sm[q], x2[parity][:, :, :]).then_inc(stored[parity], 16)

            def step(p, parity, nth, prep, cross, post):
                if not isinstance(p, int) or p + 2 < PAIRS:
                    load(p, parity, p + 2)
                if post:
                    store(p - 1, 1 - parity)

            attention_steps(sp, step)
            for k in range(2):
                sp.wait_ge(stored[k], 32 * PAIRS // 2)
            sp.wait_ge(gates_done, 1)
            sp.dma_start(table.rearrange("(b t) d -> t b d", t=P)[:, :, P:ROW], gates[:, :, :]).then_inc(gates_stored, 16)
            sp.wait_ge(scattered, 16 * SB * E)
            rows = total.rearrange("(b t) d -> t b d", t=P)
            for c in range(B // 4):
                sp.dma_start(fin[:, 4 * c:4 * c + 4, :], rows[:, 4 * c:4 * c + 4, :]).then_inc(fin_in[c], 16)
            for c in range(B // 4):
                sp.wait_ge(fin_done, 4 * (c + 1))
                sp.dma_start(out.rearrange("b t d -> t b d")[:, 4 * c:4 * c + 4, :],
                             fin[:, 4 * c:4 * c + 4, :]).then_inc(out_done, 16)
            sp.wait_ge(gates_stored, 16)
            sp.wait_ge(out_done, 16 * (B // 4))

        @block.gpsimd
        def _(pool):
            pool.memset(ident[:, :], 0.0).then_inc(consts, 1)
            pool.memset(ones[:, :], 1.0).then_inc(consts, 1)
            pool.wait_ge(consts, 1)
            pool.affine_select(out=ident[:, :], in_=ident[:, :], compare_op=ALU.not_equal, fill=1.0,
                               base=0, pattern=[[-1, P]], channel_multiplier=1).then_inc(consts, 1)
            pool.memset(mhalf[:, :], -0.5).then_inc(consts, 1)
            pool.memset(VOT[:, :, HK:HKP], 0.0).then_inc(consts, 1)
            pool.memset(pn[:, :, HK:HKP], 0.0).then_inc(consts, 1)
            pool.iota(iota[:, :], [[1, P]], base=0, channel_multiplier=0).then_inc(consts, 1)
            pool.iota(iotab[:, :], [[P, B]], base=0, channel_multiplier=0).then_inc(consts, 1)
            pool.iota(iotap[:, :], [[1, 1]], base=0, channel_multiplier=1).then_inc(consts, 1)
            pool.iota(three[:, :], [[1, 3]], base=1, channel_multiplier=0).then_inc(consts, 1)
            pool.memset(groupf[:, :], 0.0).then_inc(consts, 1)
            pool.memset(beforef[:, :], 1.0).then_inc(consts, 1)
            pool.memset(keep[:, :, :], 1.0).then_inc(consts, 1)
            pool.memset(onesb[:, :], 1.0).then_inc(consts, 1)
            pool.wait_ge(consts, 14)
            pool.memset(keep[:, :, 0:1], 0.0).then_inc(consts, 1)
            v = groupf[:, :].rearrange("p (a e) -> p a e", e=E)
            for n in range(-(P // E) + 1, P // E):
                pool.affine_select(out=v, in_=v, compare_op=ALU.not_equal, fill=1.0, base=E * n,
                                   pattern=[[-E, P // E], [-1, E]], channel_multiplier=1).then_inc(consts, 1)
                pool.wait_ge(consts, 15 + n + P // E)
            pool.affine_select(out=beforef[:, :], in_=beforef[:, :], compare_op=ALU.is_gt, fill=0.0, base=0,
                               pattern=[[1, P]], channel_multiplier=-1).then_inc(consts, 1)
            pool.tensor_copy(pcol[:, :], iotap[:, :]).then_inc(consts, 1)
            pool.wait_ge(consts, CONSTS - 1)
            pool.tensor_copy(before[:, :], beforef[:, :]).then_inc(consts, 1)
            pool.wait_ge(setup_act, 1)

            def step(p, parity, nth, prep, cross, post):
                if prep:
                    wait(pool, x_in[1 - parity], 16 * (nth + 1))
                    for e in range(2):
                        i = pool.tensor_tensor(xbo[:, e, :], xin[1 - parity][:, e, :], wvo[:, 2, :], ALU.add)
                    i.then_inc(xbo_done, 1)
                if cross:
                    for e in range(2):
                        wait(pool, crcp_done, 2 * p + e + 1)
                        pool.tensor_tensor(
                            pn[:, e, 0:HK].rearrange("p (h k) -> p h k", h=HEADS),
                            pc[:, e, :].rearrange("p (h k) -> p h k", h=HEADS),
                            crcp[:, e, :].unsqueeze(2).to_broadcast([P, HEADS, KEYS]),
                            ALU.mult).then_inc(pn_done, 1)
                if prep:
                    wait(pool, var1, p + 2)
                    pool.tensor_tensor(rs1[:, :], ve1[:, :], mhalf[:, :], ALU.pow).then_inc(rstd1, 1)
                if cross:
                    for e in range(2):
                        wait(pool, var2, 2 * p + e + 1)
                        pool.tensor_tensor(rs2[:, e:e + 1], ve2[:, e:e + 1], mhalf[:, 0:1], ALU.pow).then_inc(rstd2, 1)

            attention_steps(pool, step)

            def gather(e):
                pool.wait_ge(idx_done, e + 1)
                if e == 0:
                    pool.wait_ge(gates_stored, 16)
                    for k in range(2):
                        pool.wait_ge(stored[k], 32 * PAIRS // 2)
                if e >= 3:
                    pool.wait_ge(ye_done, 2 * (e - 2))
                for h in range(SB):
                    pool.indirect_dma_start(xg[:, e % 3, h, :], None, table,
                                            bass.IndirectOffsetOnAxis(ap=idx[:, e, h:h + 1], axis=0)
                                            ).then_inc(gathered[e % 3][h], 16)

            def scatter(e):
                if e:
                    pool.wait_ge(scattered, 16 * SB * e)
                for h in range(SB):
                    pool.wait_ge(ye_done, 2 * e + 1 + h // 4)
                    pool.indirect_dma_start(total, bass.IndirectOffsetOnAxis(ap=idx[:, e, h:h + 1], axis=0),
                                            ye[:, e % 2, h, :], None, compute_op=ALU.add).then_inc(scattered, 16)

            gather(0)
            gather(1)
            for e in range(E):
                if e + 2 < E:
                    gather(e + 2)
                scatter(e)
            for c in range(B // 4):
                pool.wait_ge(fin_var, c + 1)
                pool.tensor_tensor(rsf[:, 4 * c:4 * c + 4], vef[:, 4 * c:4 * c + 4],
                                   mhalf[:, 0:1].to_broadcast([P, 4]), ALU.pow).then_inc(fin_rstd, 1)

        @block.scalar
        def _(act):
            for k in range(1, SETUP_UNITS, 2):
                act.wait_ge(setup_full, k + 1)
                dst, n = setup_target(k)
                src = PS[:, k % 8, 0:n]
                if len(dst.shape) == 3:
                    src = src.rearrange("p (i d) -> p i d", d=P)
                s = CROSS_SCALE if 2 + W_UNITS <= k < 2 + W_UNITS + 4 else 1.0
                act.activation(dst, src, ACT.Copy, scale=s).then_inc(setup_act, 1)

            def copy(p, name, dst, src):
                ring_wait_full(act, p, name)
                act.activation(dst, src, ACT.Copy).then_inc(free[bank_of(name)], 1)

            def step(p, parity, nth, prep, cross, post):
                def heads_copy(what, u):
                    name = (what, u)
                    dst = A[1 - parity] if what == "A" else VOT
                    copy(p, name, dst[:, :, 2 * u * KEYS:(2 * u + 2) * KEYS].rearrange("p e (h k) -> p h e k", h=2),
                         ring[bank_of(name)][:, 0:4 * KEYS].rearrange("p (h e k) -> p h e k", h=2, e=2))

                def cross_exp(e):
                    wait(act, s2_free, 2 * p + e + 1)
                    act.activation(pc[:, e, :], pc[:, e, :], ACT.Exp).then_inc(cexp_done, 1)

                def cross_pT(e):
                    for g, (a, b) in enumerate(GROUPS):
                        name = ("P2T", e, g)
                        copy(p, name, pT[:, e, a * P:b * P], ring[bank_of(name)][:, 0:(b - a) * P])

                if prep:
                    copy(p, "xT", xT[:, :, :].rearrange("p e t -> p (e t)"), ring[bank_of("xT")][:, 0:2 * P])
                    copy(p, "cT", cT[:, :], ring[bank_of("cT")][:, 0:2 * KEYS])
                    ring_wait_full(act, p, "QK")
                    qk = ring[bank_of("QK")]
                    act.activation(qT[:, :, :].rearrange("p e t -> p (e t)"), qk[:, 0:2 * P], ACT.Identity,
                                   bias=bcol[:, 0:1])
                    act.activation(kT[:, :, :].rearrange("p e t -> p (e t)"), qk[:, 2 * P:4 * P], ACT.Identity,
                                   bias=bcol[:, 1:2]).then_inc(free[bank_of("QK")], 1)
                    heads_copy("A", 0)
                    heads_copy("A", 1)
                if cross:
                    cross_exp(0)
                if prep:
                    heads_copy("A", 2)
                    heads_copy("A", 3)
                    wait(act, snb_done, p + 2)
                    for e in range(2):
                        act.activation(pself[:, e, :], small[:, e * P:(e + 1) * P], ACT.Exp, bias=snb[:, e:e + 1],
                                       scale=SELF_SCALE, accum_out=ssum[:, e:e + 1]).then_inc(sexp_done, 1)
                    heads_copy("A", 4)
                if cross:
                    cross_exp(1)
                if prep:
                    heads_copy("A", 5)
                    heads_copy("A", 6)
                if cross:
                    cross_pT(0)
                if prep:
                    wait(act, self_full, 4 * (p + 1) + 2)
                    act.activation(pselfT[:, :, :].rearrange("p e t -> p (e t)"), small[:, 0:2 * P],
                                   ACT.Copy).then_inc(self_free, 1)
                    heads_copy("A", 7)
                    for u in range(5):
                        heads_copy("VOT", u)
                if cross:
                    cross_pT(1)
                if prep:
                    for u in range(5, 8):
                        heads_copy("VOT", u)
                    wait(act, self_full, 4 * (p + 1) + 4)
                    act.activation(x1T[:, :, :].rearrange("p e t -> p (e t)"), small[:, 0:2 * P],
                                   ACT.Copy).then_inc(self_free, 1)

            act.wait_ge(w_in, 16 * 15)
            attention_steps(act, step)

            act.wait_ge(g_sub, 1)
            act.activation(gates[:, :, :], gates[:, :, :], ACT.Exp).then_inc(g_exp, 1)
            for e in range(E):
                for h in range(2):
                    act.wait_ge(xeT_full, 2 * e + h + 1)
                    act.activation(xeT[:, 512 * h:512 * h + 512], PS[:, 3 + h, :], ACT.Copy).then_inc(xeT_done, 1)
                for n in range(2 * FC):
                    h, c = divmod(n, FC)
                    act.wait_ge(hid_full, 2 * FC * e + n + 1)
                    act.activation(hid[:, c, 512 * h:512 * h + 512], PS[:, HID_BANKS[(2 * FC * e + n) % 3], :], ACT.Gelu,
                                   bias=b1T[:, FC * e + c:FC * e + c + 1]).then_inc(hid_done, 1)

        @block.vector
        def _(dve):
            for k in range(0, SETUP_UNITS, 2):
                dve.wait_ge(setup_full, k + 1)
                dst, n = setup_target(k)
                src = PS[:, k % 8, 0:n]
                if len(dst.shape) == 3:
                    src = src.rearrange("p (i d) -> p i d", d=P)
                s = CROSS_SCALE if 2 + W_UNITS <= k < 2 + W_UNITS + 4 else 1.0
                dve.tensor_scalar(dst, src, s, None, ALU.mult).then_inc(setup_dve, 1)

            def step(p, parity, nth, prep, cross, post):
                def second_norm(q, e, par, earlier):
                    wait(dve, rstd2, 2 * q + e + 1)
                    wait(dve, stored[par], 32 * earlier)
                    dve.tensor_scalar(x2[par][:, e, :], r2[:, e, :], mv2[:, e, 0:1], rs2[:, e:e + 1],
                                      ALU.subtract, ALU.mult).then_inc(x2_done, 1)

                def cross_max(e):
                    wait(dve, s2_full, 2 * p + e + 1)
                    s = PS[:, 0:3, :].rearrange("p a b -> p (a b)")[:, 0:HK].rearrange("p (h k) -> p h k", h=HEADS)
                    dve.tensor_reduce(cmax[:, e, :], s, AX.X, ALU.max).then_inc(cmax_done, 1)

                def cross_sub(e):
                    wait(dve, cmax_done, 2 * p + e + 1)
                    s = PS[:, 0:3, :].rearrange("p a b -> p (a b)")[:, 0:HK].rearrange("p (h k) -> p h k", h=HEADS)
                    dve.tensor_tensor(pc[:, e, :].rearrange("p (h k) -> p h k", h=HEADS), s,
                                      cmax[:, e, :].unsqueeze(2).to_broadcast([P, HEADS, KEYS]),
                                      ALU.subtract).then_inc(s2_free, 1)

                def cross_sum(e):
                    wait(dve, cexp_done, 2 * p + e + 1)
                    dve.tensor_reduce(csum[:, e, :], pc[:, e, :].rearrange("p (h k) -> p h k", h=HEADS), AX.X,
                                      ALU.add).then_inc(csum_done, 1)
                    wait(dve, csum_done, 2 * p + e + 1)
                    dve.reciprocal(crcp[:, e, :], csum[:, e, :]).then_inc(crcp_done, 1)

                def second_stats(e):
                    name = ("AV2", e)
                    ring_wait_full(dve, p, name)
                    dve.tensor_tensor(r2[:, e, :], ring[bank_of(name)][:, 0:P], x1[parity][:, e, :],
                                      ALU.add).then_inc(free[bank_of(name)], 1)
                    ring_wait_copied(dve, p, name)
                    dve.bn_stats(st2[:, e, :], r2[:, e, :]).then_inc(ln2_steps, 1)
                    wait_apart(dve, ln2_steps, 4 * p + 2 * e + 1, passed_dve)
                    dve.bn_aggr(mv2[:, e, :], st2[:, e, :]).then_inc(ln2_steps, 1)
                    wait(dve, ln2_steps, 4 * p + 2 * e + 2)
                    dve.tensor_scalar(ve2[:, e:e + 1], mv2[:, e, 1:2], EPS, None, ALU.add).then_inc(var2, 1)

                if post:
                    second_norm(p - 1, 1, 1 - parity, nth - 1)
                    ring_wait_full(dve, p, "x2T")
                    dve.tensor_copy(x2T[:, :, :].rearrange("p e t -> p (e t)"),
                                    ring[bank_of("x2T")][:, 0:2 * P]).then_inc(free[bank_of("x2T")], 1)
                if cross:
                    cross_max(0)
                    cross_sub(0)
                if post:
                    ring_wait_full(dve, p, "LG")
                    dve.tensor_copy(logits[:, bass.ds(2 * (p - 1), 2), :].rearrange("p e n -> p (e n)"),
                                    ring[bank_of("LG")][:, 0:2 * E]).then_inc(free[bank_of("LG")], 1)
                if prep:
                    ring_wait_full(dve, p, "V")
                    dve.tensor_tensor(vs[:, :, :], ring[bank_of("V")][:, 0:2 * P].rearrange("p (e d) -> p e d", e=2),
                                      wvo[:, 1:2, :].to_broadcast([P, 2, P]), ALU.add).then_inc(free[bank_of("V")], 1)
                if cross:
                    cross_sum(0)
                    cross_max(1)
                if prep:
                    wait(dve, self_full, 4 * (p + 1) + 1)
                    dve.tensor_reduce(smax[:, :], small[:, 0:2 * P].rearrange("p (e k) -> p e k", e=2), AX.X,
                                      ALU.max).then_inc(smax_done, 1)
                    wait(dve, smax_done, p + 2)
                    dve.tensor_scalar(snb[:, :], smax[:, :], -SELF_SCALE, None, ALU.mult).then_inc(snb_done, 1)
                if cross:
                    cross_sub(1)
                    cross_sum(1)
                if prep:
                    wait(dve, sexp_done, 2 * (p + 1) + 2)
                    dve.reciprocal(srcp[:, :], ssum[:, :]).then_inc(srcp_done, 1)
                    wait(dve, srcp_done, p + 2)
                    wait(dve, xbo_done, p + 2)
                    wait(dve, self_full, 4 * (p + 1) + 3)
                    for e in range(2):
                        i = dve.scalar_tensor_tensor(out=r1[:, e, :], in0=small[:, e * P:(e + 1) * P],
                                                     scalar=srcp[:, e:e + 1], in1=xbo[:, e, :],
                                                     op0=ALU.mult, op1=ALU.add)
                    i.then_inc(self_free, 1)
                    wait(dve, self_free, 3 * (p + 1) + 2)
                    for e in range(2):
                        i = dve.bn_stats(st1[:, e, :], r1[:, e, :])
                    i.then_inc(ln1_steps, 1)
                    wait_apart(dve, ln1_steps, 2 * (p + 1) + 1, passed_dve)
                    for e in range(2):
                        i = dve.bn_aggr(mv1[:, e, :], st1[:, e, :])
                    i.then_inc(ln1_steps, 1)
                    wait(dve, ln1_steps, 2 * (p + 1) + 2)
                    dve.tensor_scalar(ve1[:, :], mv1[:, :, 1:2].rearrange("p e a -> p (e a)"), EPS, None,
                                      ALU.add).then_inc(var1, 1)
                if cross:
                    second_stats(0)
                if prep:
                    wait(dve, rstd1, p + 2)
                    for e in range(2):
                        dve.tensor_scalar(x1[1 - parity][:, e, :], r1[:, e, :], mv1[:, e, 0:1], rs1[:, e:e + 1],
                                          ALU.subtract, ALU.mult).then_inc(x1_done, 1)
                if cross:
                    second_norm(p, 0, parity, nth - parity)
                    second_stats(1)
                if prep:
                    for e in range(2):
                        for g, (a, b) in enumerate(GROUPS):
                            name = ("VO", e, g)
                            ring_wait_full(dve, p, name)
                            dve.tensor_copy(VO[:, e, a:b, :].rearrange("p c d -> p (c d)"),
                                            ring[bank_of(name)][:, 0:(b - a) * P]).then_inc(free[bank_of(name)], 1)

            attention_steps(dve, step)
            links = [0]

            def link(i):
                links[0] += 1
                i.then_inc(chain, 1)
                dve.wait_ge(chain, links[0])

            dve.wait_ge(consts, CONSTS)
            for r in range(ROUNDS):
                last = dve.tensor_scalar(pattern[:, r, :], three[:, :], 2 * (ROUNDS - 1 - r), None, ALU.logical_shift_left)
            link(last)
            ring_wait_copied(dve, PAIRS, "LG")
            link(dve.tensor_reduce(gmax[:, :], logits[:, :, :], AX.X, ALU.max))
            dve.tensor_tensor(gates[:, :, :], logits[:, :, :], gmax[:, :].unsqueeze(2).to_broadcast([P, B, E]),
                              ALU.subtract).then_inc(g_sub, 1)
            dve.wait_ge(g_exp, 1)
            link(dve.tensor_reduce(gsum[:, :], gates[:, :, :], AX.X, ALU.add))
            link(dve.reciprocal(grcp[:, :], gsum[:, :]))
            dve.tensor_tensor(gates[:, :, :], gates[:, :, :], grcp[:, :].unsqueeze(2).to_broadcast([P, B, E]),
                              ALU.mult).then_inc(gates_done, 1)
            dve.memset(thr[:, :], 0)
            dve.wait_ge(gatesT_full, 1)
            link(dve.tensor_copy(gatesT[:, :], PS[:, 0, 0:2 * P]))

            for r in range(ROUNDS):
                now = pattern[:, 0, :] if r == 0 else cand[:, r % 2, :]
                for j in range(3):
                    i = dve.tensor_scalar(above[:, j, :], gatesT[:, :], now[:, j:j + 1].bitcast(F32), None,
                                          ALU.is_ge, ALU.add, accum_out=count[:, r % 2, j:j + 1])
                i.then_inc(counted, 1)
                dve.wait_ge(summed, r + 1)
                link(dve.tensor_scalar(passed[:, :], PS[:, 1, 0:3], float(TOPK), None, ALU.is_ge, ALU.add,
                                       accum_out=npassed[:, :]))
                link(dve.tensor_scalar(bits[:, :], npassed[:, :], float(4 ** (ROUNDS - 1 - r)), None, ALU.mult))
                if r + 1 < ROUNDS:
                    dve.scalar_tensor_tensor(out=cand[:, (r + 1) % 2, :], in0=pattern[:, r + 1, :],
                                             scalar=thr[:, r % 2:r % 2 + 1], in1=bits[:, :].to_broadcast([P, 3]),
                                             op0=ALU.bitwise_or, op1=ALU.bitwise_or)
                link(dve.tensor_tensor(thr[:, (r + 1) % 2:(r + 1) % 2 + 1], thr[:, r % 2:r % 2 + 1], bits[:, :],
                                       ALU.bitwise_or))
            dve.tensor_scalar(thr8[:, :], ident[0:E, 0:E], thr[0:E, ROUNDS % 2:ROUNDS % 2 + 1].bitcast(F32), None,
                              ALU.mult).then_inc(thr8_done, 1)
            dve.wait_ge(thrb_full, 1)
            link(dve.tensor_copy(thrb[:, :], PS[:, 1, 8:8 + E]))
            g = gates[:, :, :].rearrange("p b e -> p e b")
            t = thrb[:, :].unsqueeze(2).to_broadcast([P, E, B])
            dve.tensor_tensor(taken[:, 0, :, :], g, t, ALU.is_gt)
            dve.tensor_tensor(taken[:, 1, :, :], g, t, ALU.is_equal).then_inc(taken_done, 1)
            dve.wait_ge(prefix_full, 1)
            flat = "p a e b -> p (a e b)"
            link(dve.tensor_tensor_scan(totals[:, :], keep[:, :, :].rearrange("p n b -> p (n b)"), PS[:, 3, :], 0.0,
                                        ALU.mult, ALU.add))
            link(dve.tensor_tensor(slot[:, :, :, :].rearrange(flat), PS[:, 2, :], totals[:, :], ALU.add))
            link(dve.tensor_tensor(slot2[:, :, :, :].rearrange(flat), slot[:, :, :, :].rearrange(flat), PS[:, 3, :],
                                   ALU.subtract))
            n_above = totals[:, :].rearrange("p (a e b) -> p a e b", a=2, e=E)[:, 0, :, B - 1:B].to_broadcast([P, E, B])
            link(dve.tensor_tensor(slot2[:, 1, :, :], slot2[:, 1, :, :], n_above, ALU.add))
            link(dve.scalar_tensor_tensor(out=slot[:, :, :, :].rearrange(flat), in0=slot2[:, :, :, :].rearrange(flat),
                                          scalar=-NONE, in1=taken[:, :, :, :].rearrange(flat), op0=ALU.add, op1=ALU.mult))
            link(dve.scalar_tensor_tensor(out=sloti[:, :, :], in0=slot[:, 0, :, :], scalar=NONE, in1=slot[:, 1, :, :],
                                          op0=ALU.add, op1=ALU.add))
            dve.tensor_scalar(slotlo[:, :, :], sloti[:, :, :], P - 1, None, ALU.bitwise_and)
            link(dve.tensor_scalar(slothi[:, :, :], sloti[:, :, :], 7, None, ALU.logical_shift_right))

            def one_hots(e):
                if e:
                    dve.wait_ge(list_full, e)
                link(dve.tensor_tensor(hot8[:, :, :], slothi[:, e, :].unsqueeze(2).to_broadcast([P, B, SB]),
                                       iota[:, 0:SB].unsqueeze(1).to_broadcast([P, B, SB]), ALU.is_equal))
                dve.tensor_tensor(tokens[:, :, :, 0], hot8[:, :, :],
                                  iotab[:, :].unsqueeze(2).to_broadcast([P, B, SB]), ALU.mult)
                dve.tensor_scalar(tokens[:, :, :, 1], hot8[:, :, :], pcol[:, 0:1], None, ALU.mult).then_inc(tokens_done, 1)
                for q in range(4):
                    b = B // 4 * q
                    dve.tensor_tensor(onehot[:, b:b + B // 4, :], iota[:, :].unsqueeze(1).to_broadcast([P, B // 4, P]),
                                      slotlo[:, e, b:b + B // 4].unsqueeze(2).to_broadcast([P, B // 4, P]),
                                      ALU.is_equal).then_inc(onehot_done, 1)

            def make_idx(e):
                dve.wait_ge(list_full, e + 1)
                with nc.allow_low_precision(reason="numbers of tokens are whole and below 2 ** 24"):
                    dve.tensor_reduce(idx[:, e, :], PS[:, 7, 0:2 * SB].rearrange("p (s a) -> p s a", a=2), AX.X,
                                      ALU.add).then_inc(idx_done, 1)

            def results(e, h):
                if e >= 2:
                    dve.wait_ge(scattered, 16 * SB * (e - 1))
                dve.wait_ge(ye_full, 2 * e + h + 1)
                dve.tensor_tensor(yb[:, 4 * h:4 * h + 4, :], PS[:, 1 + h, :].rearrange("p (s d) -> p s d", d=P),
                                  b2b[:, e:e + 1, :].to_broadcast([P, 4, P]), ALU.add).then_inc(ye_added, 1)
                dve.wait_ge(ye_added, 2 * e + h + 1)
                for s in range(4 * h, 4 * h + 4):
                    dve.wait_ge(gathered[e % 3][s], 16 * (e // 3 + 1))
                dve.tensor_tensor(ye[:, e % 2, 4 * h:4 * h + 4, :], yb[:, 4 * h:4 * h + 4, :],
                                  xg[:, e % 3, 4 * h:4 * h + 4, P + e:P + e + 1].to_broadcast([P, 4, P]),
                                  ALU.mult).then_inc(ye_done, 1)

            for e in range(3):
                one_hots(e)
                make_idx(e)
            for e in range(E):
                if e + 3 < E:
                    one_hots(e + 3)
                results(e, 0)
                if e + 3 < E:
                    make_idx(e + 3)
                results(e, 1)

            def fin_norm(c):
                dve.wait_ge(fin_rstd, c + 1)
                for b in range(4 * c, 4 * c + 4):
                    dve.tensor_scalar(fin[:, b, :], fin[:, b, :], mvf[:, b, 0:1], rsf[:, b:b + 1],
                                      ALU.subtract, ALU.mult).then_inc(fin_done, 1)

            for c in range(B // 4):
                dve.wait_ge(fin_in[c], 16)
                for b in range(4 * c, 4 * c + 4):
                    i = dve.bn_stats(stf[:, b, :], fin[:, b, :])
                link(i)
                for b in range(4 * c, 4 * c + 4):
                    i = dve.bn_aggr(mvf[:, b, :], stf[:, b, :])
                link(i)
                dve.tensor_scalar(vef[:, 4 * c:4 * c + 4], mvf[:, 4 * c:4 * c + 4, 1:2].rearrange("p b a -> p (b a)"), EPS,
                                  None, ALU.add).then_inc(fin_var, 1)
                if c:
                    fin_norm(c - 1)
            fin_norm(B // 4 - 1)

        @block.tensor
        def _(pe):
            def setup_unit(k):
                if k >= 8:
                    pe.wait_ge((setup_dve, setup_act)[k % 2], (k - 8) // 2 + 1)
                return PS[:, k % 8, :]

            pe.wait_ge(consts, 4)
            pe.wait_ge(w_in, 16 * 15)
            bank = setup_unit(0)
            for j, w in enumerate((0, 1, 3)):
                i = pe.transpose(bank[:, j * P:(j + 1) * P], wself[:, w, :], ident[:, :])
            i.then_inc(setup_full, 1)
            bank = setup_unit(1)
            pe.wait_ge(setup_dve, 1)
            pe.matmul(bank[:, 0:P], wself[:, 2, :], wT[:, 2, :], start=True, stop=True)
            pe.matmul(bank[:, P:2 * P], bcol[:, 2:3].to_broadcast([P, P]), wT[:, 2, :], start=True, stop=True)
            pe.matmul(bank[:, 2 * P:3 * P], ones[0:1, :], brow[0:1, 0:P], start=True, stop=True).then_inc(setup_full, 1)
            for k in range(2, 2 + W_UNITS):
                bank = setup_unit(k)
                w, g = divmod(k - 2, 2)
                for j in range(4):
                    c = 4 * g + j
                    i = pe.transpose(bank[:, j * P:(j + 1) * P], wheads[:, w, c * P:(c + 1) * P], ident[:, :])
                i.then_inc(setup_full, 1)
            for k in range(2 + W_UNITS, 2 + W_UNITS + 8):
                bank = setup_unit(k)
                m, g = divmod(k - 2 - W_UNITS, 4)
                pe.wait_ge(setup_dve, 1 + W_UNITS // 2)
                pe.wait_ge(setup_act, 1 + W_UNITS // 2)
                lo = DK * (g % 2)
                for j in range(4):
                    c = 4 * (g // 2) + j
                    lhsT = wheadsT[lo:lo + DK, 1 if m == 0 else 2, c, :]
                    rhs = wheadsT[lo:lo + DK, 0, c, :] if m == 0 else won[lo:lo + DK, c, :]
                    i = pe.matmul(bank[:, j * P:(j + 1) * P], lhsT, rhs, start=True, stop=True)
                i.then_inc(setup_full, 1)
            k = 2 + W_UNITS + 8
            pe.transpose(setup_unit(k)[:, 0:E * FC], b1n[:, :], ident[0:E * FC, 0:E * FC]).then_inc(setup_full, 1)
            pe.wait_ge(consts, CONSTS)
            pe.transpose(setup_unit(k + 1)[:, 0:P], groupf[:, :], ident[:, :]).then_inc(setup_full, 1)
            for j in range(2):
                pe.matmul(setup_unit(k + 2 + j)[:, :], ones[0:1, :], brow[0:1, P + 512 * j:P + 512 * (j + 1)],
                          start=True, stop=True).then_inc(setup_full, 1)
            pe.wait_ge(setup_dve, SETUP_UNITS // 2)
            pe.wait_ge(setup_act, SETUP_UNITS // 2)
            pe.wait_ge(consts, 6)

            def step(p, parity, nth, prep, cross, post):
                def unit(name):
                    ring_wait_free(pe, p, name)
                    return ring[bank_of(name)]

                def done(i, name):
                    i.then_inc(full[bank_of(name)], 1)

                def heads(what, u):
                    name = (what, u)
                    bank = unit(name)
                    w = MT if what == "A" else NN
                    for j in range(2):
                        i = pe.matmul(bank[:, j * 2 * KEYS:(j + 1) * 2 * KEYS], w[:, 2 * u + j, :], cT[:, :],
                                      start=True, stop=True)
                    done(i, name)

                def cross_scores(e):
                    wait(pe, s2_free, 2 * p + e)
                    for n in range(3):
                        a, b = n * 512, min((n + 1) * 512, HK)
                        i = pe.matmul(PS[:, n, 0:b - a], x1T[:, e, :], A[parity][:, e, a:b], start=True, stop=True)
                    i.then_inc(s2_full, 1)

                def cross_pT(e):
                    wait(pe, pn_done, 2 * p + e + 1)
                    for g, (a, b) in enumerate(GROUPS):
                        name = ("P2T", e, g)
                        bank = unit(name)
                        for c in range(a, b):
                            i = pe.transpose(bank[:, (c - a) * P:(c - a + 1) * P], pn[:, e, c * P:(c + 1) * P], ident[:, :])
                        done(i, name)

                def cross_out(e):
                    name = ("AV2", e)
                    bank = unit(name)
                    if e == 0:
                        ring_wait_copied(pe, p - 1, ("VO", 1, 2))
                    ring_wait_copied(pe, p, ("P2T", e, 0))
                    ring_wait_copied(pe, p, ("P2T", e, 1))
                    ring_wait_copied(pe, p, ("P2T", e, 2))
                    for c in range(CH):
                        i = pe.matmul(bank[:, 0:P], pT[:, e, c * P:(c + 1) * P], VO[:, e, c, :],
                                      start=(c == 0), stop=(c == CH - 1))
                    done(i, name)

                if cross:
                    wait(pe, self_free, 3 * p + 3)
                    cross_scores(0)
                if prep:
                    wait(pe, x_in[1 - parity], 16 * (nth + 1))
                    wait(pe, c_in[1 - parity], 16 * (nth + 1))
                    bank = unit("xT")
                    for e in range(2):
                        i = pe.transpose(bank[:, e * P:(e + 1) * P], xin[1 - parity][:, e, :], ident[:, :])
                    done(i, "xT")
                    bank = unit("cT")
                    for e in range(2):
                        i = pe.transpose(bank[:, e * KEYS:(e + 1) * KEYS], cin[1 - parity][:, e, :], ident[0:KEYS, 0:KEYS])
                    done(i, "cT")
                if post:
                    wait(pe, x2_done, 2 * (p - 1) + 2)
                    bank = unit("x2T")
                    for e in range(2):
                        i = pe.transpose(bank[:, e * P:(e + 1) * P], x2[1 - parity][:, e, :], ident[:, :])
                    done(i, "x2T")
                if prep:
                    bank = unit("QK")
                    ring_wait_copied(pe, p, "xT")
                    for j in range(2):
                        i = pe.matmul(bank[:, j * 2 * P:(j + 1) * 2 * P], wT[:, j, :],
                                      xT[:, :, :].rearrange("p e t -> p (e t)"), start=True, stop=True)
                    done(i, "QK")
                if post:
                    bank = unit("LG")
                    ring_wait_copied(pe, p, "x2T")
                    for e in range(2):
                        i = pe.matmul(bank[:, e * E:(e + 1) * E], x2T[:, e, :], wr[:, :], start=True, stop=True)
                    done(i, "LG")
                if prep:
                    bank = unit("V")
                    for e in range(2):
                        i = pe.matmul(bank[:, e * P:(e + 1) * P], xT[:, e, :], wvo[:, 0, :], start=True, stop=True)
                    done(i, "V")
                    ring_wait_copied(pe, p, "cT")
                    for u in range(3):
                        heads("A", u)
                if cross:
                    cross_scores(1)
                if prep:
                    wait(pe, self_free, 3 * (p + 1))
                    ring_wait_copied(pe, p, "QK")
                    for e in range(2):
                        i = pe.matmul(small[:, e * P:(e + 1) * P], qT[:, e, :], kT[:, e, :], start=True, stop=True)
                    i.then_inc(self_full, 1)
                    for u in range(3, 7):
                        heads("A", u)
                if cross:
                    cross_pT(0)
                if prep:
                    wait(pe, sexp_done, 2 * (p + 1) + 2)
                    for e in range(2):
                        i = pe.transpose(small[:, e * P:(e + 1) * P], pself[:, e, :], ident[:, :])
                    i.then_inc(self_full, 1)
                    heads("A", 7)
                    heads("VOT", 0)
                if cross:
                    cross_out(0)
                if prep:
                    wait(pe, self_free, 3 * (p + 1) + 1)
                    ring_wait_copied(pe, p, "V")
                    for e in range(2):
                        i = pe.matmul(small[:, e * P:(e + 1) * P], pselfT[:, e, :], vs[:, e, :], start=True, stop=True)
                    i.then_inc(self_full, 1)
                    for u in range(1, 5):
                        heads("VOT", u)
                if cross:
                    cross_pT(1)
                if prep:
                    for u in range(5, 8):
                        heads("VOT", u)
                if cross:
                    cross_out(1)
                if prep:
                    wait(pe, x1_done, 2 * (p + 1) + 2)
                    for e in range(2):
                        i = pe.transpose(small[:, e * P:(e + 1) * P], x1[1 - parity][:, e, :], ident[:, :])
                    i.then_inc(self_full, 1)
                    for u in range(8):
                        ring_wait_copied(pe, p, ("VOT", u)) if u >= 4 else None
                    for e in range(2):
                        for g, (a, b) in enumerate(GROUPS):
                            name = ("VO", e, g)
                            bank = unit(name)
                            for c in range(a, b):
                                i = pe.transpose(bank[:, (c - a) * P:(c - a + 1) * P], VOT[:, e, c * P:(c + 1) * P], ident[:, :])
                            done(i, name)

            attention_steps(pe, step)

            pe.wait_ge(gates_done, 1)
            for k in range(RING_BANKS):
                n = sum(1 for j in range(len(UNITS)) if j % RING_BANKS == k) * PAIRS
                pe.wait_ge(free[k], n)
            for g in range(2):
                i = pe.transpose(PS[:, 0, g * P:(g + 1) * P],
                                 gates[:, B // 2 * g:B // 2 * (g + 1), :].rearrange("p b e -> p (b e)"), ident[:, :])
            i.then_inc(gatesT_full, 1)
            for r in range(ROUNDS):
                pe.wait_ge(counted, r + 1)
                pe.matmul(PS[:, 1, 0:3], group[:, :], count[:, r % 2, :], start=True, stop=True).then_inc(summed, 1)
            pe.wait_ge(thr8_done, 1)
            pe.matmul(PS[:, 1, 8:8 + E], ones[0:E, :], thr8[:, :], start=True, stop=True).then_inc(thrb_full, 1)
            pe.wait_ge(taken_done, 1)
            t = taken[:, :, :, :].rearrange("p a e b -> p (a e b)")
            pe.matmul(PS[:, 2, :], before[:, :], t, start=True, stop=True)
            pe.matmul(PS[:, 3, :], onesb[:, :], t, start=True, stop=True).then_inc(prefix_full, 1)

            def make_list(e):
                pe.wait_ge(tokens_done, e + 1)
                if e:
                    pe.wait_ge(idx_done, e)
                for b in range(B):
                    if b % (B // 4) == 0:
                        pe.wait_ge(onehot_done, 4 * e + b // (B // 4) + 1)
                    i = pe.matmul(PS[:, 7, 0:2 * SB], onehot[:, b, :], tokens[:, b, :, :].rearrange("p s a -> p (s a)"),
                                  start=(b == 0), stop=(b == B - 1))
                i.then_inc(list_full, 1)

            def transpose_rows(e):
                for h in range(2):
                    if e:
                        pe.wait_ge(xeT_done, 2 * (e - 1) + h + 1)
                    for s in range(4):
                        pe.wait_ge(gathered[e % 3][4 * h + s], 16 * (e // 3 + 1))
                        i = pe.transpose(PS[:, 3 + h, s * P:(s + 1) * P], xg[:, e % 3, 4 * h + s, 0:P], ident[:, :])
                    i.then_inc(xeT_full, 1)

            def hidden(e):
                for n in range(2 * FC):
                    h, c = divmod(n, FC)
                    k = 2 * FC * e + n
                    if c == 0:
                        pe.wait_ge(xeT_done, 2 * e + h + 1)
                    if k >= 3:
                        pe.wait_ge(hid_done, k - 2)
                    pe.matmul(PS[:, HID_BANKS[k % 3], :], w1[:, e, c * P:(c + 1) * P], xeT[:, 512 * h:512 * h + 512],
                              start=True, stop=True).then_inc(hid_full, 1)

            def second_layer(e, h):
                pe.wait_ge(hid_done, 2 * FC * e + FC * (h + 1))
                if e:
                    pe.wait_ge(ye_added, 2 * (e - 1) + h + 1)
                for s in range(4):
                    for c in range(FC):
                        i = pe.matmul(PS[:, 1 + h, s * P:(s + 1) * P], hid[:, c, (4 * h + s) * P:(4 * h + s + 1) * P],
                                      w2[:, e, c, :], start=(c == 0), stop=(c == FC - 1))
                i.then_inc(ye_full, 1)

            for e in range(3):
                make_list(e)
            pe.wait_ge(moe_in, 32)
            transpose_rows(0)
            for e in range(E):
                hidden(e)
                second_layer(e, 0)
                if e + 1 < E:
                    transpose_rows(e + 1)
                if e + 3 < E:
                    make_list(e + 3)
                second_layer(e, 1)


_INS = ["x", "ctx_1024", "L0_attn_Wq", "L0_attn_bq", "L0_attn_Wk", "L0_attn_bk", "L0_attn_Wv", "L0_attn_bv",
        "L0_attn_Wo", "L0_attn_bo", "L0_xattn_W_Q", "L0_xattn_W_K", "L0_xattn_W_V", "L0_xattn_W_O",
        "L0_ffn_Wr", "L0_ffn_W1", "L0_ffn_b1", "L0_ffn_W2", "L0_ffn_b2"]


def kernel(**inputs):
    import numpy as _np
    import concourse.bacc as _bacc
    from concourse import mybir as _mybir
    from concourse.bass_utils import run_bass_kernel_spmd as _run

    nc = _bacc.Bacc("TRN2", target_bir_lowering=False, num_devices=1)
    arrays, args = {}, []
    for name in _INS:
        a = _np.ascontiguousarray(inputs[name])
        arrays[f"in_{name}"] = a
        args.append(nc.dram_tensor(f"in_{name}", a.shape, _mybir.dt.from_np(a.dtype), kind="ExternalInput").ap())
    args.append(nc.dram_tensor("out_x", (B, P, P), F32, kind="ExternalOutput").ap())
    decoder_layer(nc, *args)
    r = _run(nc, [arrays], core_ids=[0])
    return r.results[0]["out_x"]
```

```python
from contextlib import ExitStack

import concourse.bass as bass
from concourse import mybir

ALU = mybir.AluOpType
ACT = mybir.ActivationFunctionType
AX = mybir.AxisListType
F32 = mybir.dt.float32
BF16 = mybir.dt.bfloat16
I32 = mybir.dt.int32

P = 128
B = 32
PAIRS = B // 2
KEYS = 77
HEADS = 16
DK = 64
HK = HEADS * KEYS
CH = -(-HK // P)
HKP = CH * P
E = 8
F = 512
FC = F // P
EPS = 1e-5
SELF_SCALE = 1.0 / 8.0
CROSS_SCALE = 1.0 / 8.0
ROW = P + E

RING_BANKS = 4
HEAD_UNITS = -(-HEADS // 3)
UNITS = (
    [("QK", "prep"), ("V", "prep"), (("A", 0), "prep"), (("A", 1), "prep"), ("x2T", "post"), (("A", 2), "prep"),
     (("A", 3), "prep"), ("LG", "post"), (("A", 4), "prep"), (("A", 5), "prep")]
    + [(("VOT", u), "prep") for u in range(3)]
    + [(("P2T", 0, g), "cross") for g in range(3)]
    + [(("VOT", u), "prep") for u in range(3, 6)]
    + [("xT", "ahead"), ("cT", "ahead"), (("AV2", 0), "cross")]
    + [(("P2T", 1, g), "cross") for g in range(3)]
    + [(("VO", 0, g), "prep") for g in range(3)]
    + [(("AV2", 1), "cross")]
    + [(("VO", 1, g), "prep") for g in range(3)]
)
assert len(UNITS) % RING_BANKS == 0
SLOT = {name: k for k, (name, _) in enumerate(UNITS)}
LEAD = {"ahead": 2, "prep": 1, "cross": 0, "post": -1}
GROUPS = [(0, 4), (4, 8), (8, CH)]
TOKENS = B * P
TOPK = max(4, -(-2 * TOKENS // E))
SB = TOPK // P
NONE = float(TOKENS)
WARM = {"start": 12, ("fold", 0, 0): 3, ("turn", 0, 1): 10, ("turn", 1, 1): 3}
ROUNDS = 15


FOUR = 0x40800000
NBIT = 21


def answer_shift(r):
    return 2 * (ROUNDS - 1 - r) - NBIT


LEFTS = sum(answer_shift(r) > 0 for r in range(ROUNDS))


def shifted_four(r):
    k = answer_shift(r)
    v = FOUR << k & 0xFFFFFFFF if k >= 0 else FOUR >> -k
    return v - (1 << 32) if v >> 31 else v


def clip(n, most):
    return max(0, min(n, most)) if isinstance(n, int) else n


def bank_of(name):
    return SLOT[name] % RING_BANKS


def fills_before(step, name):
    k = SLOT[name]
    total = 0
    for j, (_, stage) in enumerate(UNITS):
        if j % RING_BANKS == k % RING_BANKS:
            total = total + clip(step + LEAD[stage] + (1 if j < k else 0), PAIRS)
    return total


def wait(eng, sem, count):
    if isinstance(count, int) and count <= 0:
        return
    eng.wait_ge(sem, count)


def wait_apart(eng, sem, count, passed):
    wait(eng, sem, count)
    if not isinstance(count, int):
        eng.sem_inc(passed, 1)


def heads_of(u):
    return range(3 * u, min(3 * u + 3, HEADS))


def attention_steps(eng, step):
    def at(p, parity, nth):
        steady = not isinstance(p, int)
        step(p, parity, nth, steady or p + 2 < PAIRS, steady or -1 <= p < PAIRS - 1, steady or 0 <= p < PAIRS,
             steady or p > 0)

    at(-2, 0, -1)
    at(-1, 1, 0)
    at(0, 0, 0)
    with eng.Fori(0, (PAIRS - 4) // 2) as i:
        at(2 * i + 1, 1, i + 1)
        at(2 * i + 2, 0, i + 1)
    for p in range(PAIRS - 3, PAIRS + 1):
        at(p, p % 2, (p + 1) // 2)


def decoder_layer(nc, x, ctx_1024, Wq, bq, Wk, bk, Wv, bv, Wo, bo, W_Q, W_K, W_V, W_O, Wr, W1, b1, W2, b2, out):
    ctx = ExitStack()
    with ctx:
        def sb(name, shape, dt=F32):
            return ctx.enter_context(nc.sbuf_tensor(name, shape, dt))

        def sem(name):
            return ctx.enter_context(nc.semaphore(name))

        PS = ctx.enter_context(nc.psum_tensor("PS", [P, 8, 512], F32))
        ring = [PS[:, 3 + k, :] for k in range(RING_BANKS)]
        small = PS[:, 7, :]

        ident = sb("ident", [P, P])
        ones = sb("ones", [P, P])
        mhalf = sb("mhalf", [P, 2])
        wself = sb("wself", [P, 4, P])
        brow = sb("brow", [1, P + E * P])
        bcol = sb("bcol", [P, 3])
        shared1 = sb("shared1", [P, 3 * SB * ROW])
        wheads = shared1[:, 0:3 * HEADS * DK].rearrange("p (w n) -> p w n", w=3)
        xg = shared1[:, :].rearrange("p (b s n) -> p b s n", b=3, s=SB)
        won = sb("won", [P, HEADS // 2, P])
        wT = sb("wT", [P, 3, P])
        wvo = sb("wvo", [P, 2, P])
        wheadsT = sb("wheadsT", [P, 3, HEADS // 2, P])
        shared2 = sb("shared2", [P, 2 * HEADS, P])
        MT = shared2[:, 0:HEADS, :]
        NN = shared2[:, HEADS:2 * HEADS, :]
        fin = shared2
        wr = sb("wr", [P, E])
        b1n = sb("b1n", [E * FC, P])
        b1T = sb("b1T", [P, E * FC])
        b2b = sb("b2b", [P, E, P])
        w1 = sb("w1", [P, E, F])
        w2 = sb("w2", [P, E, FC, P])
        xin = [sb(f"xin{k}", [P, 2, P]) for k in range(2)]
        cin = [sb(f"cin{k}", [KEYS, 2, P]) for k in range(2)]
        xbo = sb("xbo", [P, 2, P])
        xT = sb("xT", [P, 2, P])
        cT = sb("cT", [P, 2 * KEYS])
        qT = sb("qT", [P, 2, P])
        kT = sb("kT", [P, 2, P])
        vs = sb("vs", [P, 2, P])
        smax = sb("smax", [P, 2])
        snb = sb("snb", [P, 2])
        pself = sb("pself", [P, 2, P])
        ssum = sb("ssum", [P, 2])
        srcp = sb("srcp", [P, 2])
        pselfT = sb("pselfT", [P, 2, P])
        r1 = sb("r1", [P, 2, P])
        st1 = sb("st1", [P, 2, 6])
        mv1 = sb("mv1", [P, 2, 2])
        ve1 = sb("ve1", [P, 2])
        rs1 = sb("rs1", [P, 2])
        x1 = [sb(f"x1_{k}", [P, 2, P]) for k in range(2)]
        x1T = sb("x1T", [P, 2, P])
        shared3 = sb("shared3", [P, 4 * HK])
        A = [shared3[:, k * 2 * HK:(k + 1) * 2 * HK].rearrange("p (e n) -> p e n", e=2)
             for k in range(2)]
        hid = shared3[:, 0:FC * TOPK].rearrange("p (c t) -> p c t", c=FC)
        VOT = sb("VOT", [P, 2, HKP])
        VO = sb("VO", [P, 2, CH, P])
        pc = sb("pc", [P, 2, HK])
        onehot = pc[:, :, :].rearrange("p e n -> p (e n)")[:, 0:B * P // 2].bitcast(BF16).rearrange(
            "p (b s) -> p b s", b=B)
        pn = sb("pn", [P, 2, HKP])
        ye = pn[:, :, :].rearrange("p e n -> p (e n)")[:, 0:2 * TOPK].rearrange("p (b s d) -> p b s d", b=2, s=SB)
        pT = sb("pT", [P, 2, HKP])
        xeT = pT[:, 0, 0:TOPK]
        cmax = sb("cmax", [P, 2, HEADS])
        csum = sb("csum", [P, 2, HEADS])
        crcp = sb("crcp", [P, 2, HEADS])
        r2 = sb("r2", [P, 2, P])
        st2 = sb("st2", [P, 2, 6])
        mv2 = sb("mv2", [P, 2, 2])
        ve2 = sb("ve2", [P, 2])
        rs2 = sb("rs2", [P, 2])
        x2 = [sb(f"x2_{k}", [P, 2, P]) for k in range(2)]
        x2T = sb("x2T", [P, 2, P])
        logits = sb("logits", [P, B, E])
        gates = sb("gates", [P, B, E])
        gmax = sb("gmax", [P, B])
        gsum = sb("gsum", [P, B])
        grcp = sb("grcp", [P, B])
        gatesT = sb("gatesT", [P, 2 * P])
        above = sb("above", [P, 3, 2 * P], BF16)
        count = sb("count", [P, 2, 3 + 4], BF16)
        group = sb("group", [P, P], BF16)
        groupf = sb("groupf", [P, P])
        passed = sb("passed", [P, 3 + 4])
        npassed = sb("npassed", [P, 1])
        nextpat = sb("nextpat", [P, 4], I32)
        three = sb("three", [P, 4], I32)
        shifts = sb("shifts", [P, ROUNDS], I32)
        pattern = sb("pattern", [P, ROUNDS + 1, 4], I32)
        cand = sb("cand", [P, 2, 4], I32)
        thr8 = sb("thr8", [E, E])
        thrb = sb("thrb", [P, E])
        before = sb("before", [P, P], BF16)
        beforef = sb("beforef", [P, P])
        onesb = sb("onesb", [P, P], BF16)
        keep = sb("keep", [P, E, 2 * B])
        taken = sb("taken", [P, E, 2, B], BF16)
        totals = sb("totals", [P, 2 * E * B])
        slot = sb("slot", [P, E, 2, B])
        slot2 = sb("slot2", [P, E, 2, B])
        sloti = sb("sloti", [P, E, B], I32)
        slotlo = sb("slotlo", [P, E, B], I32)
        slothi = sb("slothi", [P, E, B], I32)
        iota = sb("iota", [P, P], I32)
        iotab = sb("iotab", [P, B], I32)
        iotap = sb("iotap", [P, 1], I32)
        pcol = sb("pcol", [P, 1])
        hot8 = sb("hot8", [P, B, SB], BF16)
        tokens = sb("tokens", [P, B, SB, 2], BF16)
        idx = sb("idx", [P, E, SB], I32)
        yb = VO[:, 0, 0:SB, :]
        stf = sb("stf", [P, B, 6])
        mvf = sb("mvf", [P, B, 2])
        vef = sb("vef", [P, B])
        rsf = sb("rsf", [P, B])
        nmf = sb("nmf", [P, B])

        self_in = sem("self_in")
        heads_in = [sem(f"heads_in{k}") for k in range(3)]
        wo_in = sem("wo_in")
        small_in = sem("small_in")
        route_in = sem("route_in")
        x_in = [sem(f"x_in{k}") for k in range(2)]
        c_in = [sem(f"c_in{k}") for k in range(2)]
        consts = sem("consts")
        setup_full = sem("setup_full")
        setup_dve = sem("setup_dve")
        setup_act = sem("setup_act")
        full = [sem(f"ring_full{k}") for k in range(RING_BANKS)]
        free = [sem(f"ring_free{k}") for k in range(RING_BANKS)]
        self_full = sem("self_full")
        self_free = sem("self_free")
        s2_full = sem("s2_full")
        s2_free = sem("s2_free")
        cmax_done = sem("cmax_done")
        cexp_done = sem("cexp_done")
        csum_done = sem("csum_done")
        crcp_done = sem("crcp_done")
        pn_done = sem("pn_done")
        smax_done = sem("smax_done")
        snb_done = sem("snb_done")
        sexp_done = sem("sexp_done")
        srcp_done = sem("srcp_done")
        xbo_done = sem("xbo_done")
        ln1_steps = sem("ln1_steps")
        ln2_steps = sem("ln2_steps")
        r2_done = sem("r2_done")
        var1 = sem("var1")
        rstd1 = sem("rstd1")
        var2 = sem("var2")
        rstd2 = sem("rstd2")
        x1_done = sem("x1_done")
        x2_done = sem("x2_done")
        stored = [sem(f"stored{k}") for k in range(2)]
        passed_dve = sem("passed_dve")
        passed_sp = sem("passed_sp")
        chain = sem("chain")
        attended = sem("attended")
        moe_in = sem("moe_in")
        g_sub = sem("g_sub")
        g_exp = sem("g_exp")
        gates_done = sem("gates_done")
        late_full = sem("late_full")
        late_done = sem("late_done")
        gates_stored = sem("gates_stored")
        gatesT_full = sem("gatesT_full")
        counted = sem("counted")
        summed = sem("summed")
        thr8_done = sem("thr8_done")
        thrb_full = sem("thrb_full")
        taken_done = sem("taken_done")
        prefix_full = sem("prefix_full")
        onehot_done = sem("onehot_done")
        tokens_done = sem("tokens_done")
        list_full = sem("list_full")
        idx_done = sem("idx_done")
        gathered = [[sem(f"gathered{b}_{h}") for h in range(SB)] for b in range(3)]
        xeT_full = sem("xeT_full")
        xeT_done = sem("xeT_done")
        hid_full = sem("hid_full")
        hid_done = sem("hid_done")
        ye_full = sem("ye_full")
        ye_added = sem("ye_added")
        ye_done = sem("ye_done")
        scattered = sem("scattered")
        fin_in = [sem(f"fin_in{c}") for c in range(B // 4)]
        fin_var = sem("fin_var")
        fin_rstd = sem("fin_rstd")
        fin_shifted = sem("fin_shifted")
        fin_done = sem("fin_done")
        out_done = sem("out_done")
        table = nc.dram_tensor("table", [TOKENS, ROW], F32, kind="Internal").ap()
        total = nc.dram_tensor("total", [TOKENS, P], F32, kind="Internal").ap()

        x_pairs = x.rearrange("(q e) t d -> q t e d", e=2)
        c_pairs = ctx_1024.rearrange("(q e) s d -> q s e d", e=2)

        def ring_wait_free(eng, step, name):
            wait(eng, free[bank_of(name)], fills_before(step, name))

        def ring_wait_full(eng, step, name):
            wait(eng, full[bank_of(name)], fills_before(step, name) + 1)

        def ring_wait_copied(eng, step, name):
            wait(eng, free[bank_of(name)], fills_before(step, name) + 1)

        HID_BANKS = (5, 6, 0)
        CONSTS = 19 + 2 * (P // E) - 1 + 3

        SETUP = ([("self", 0, 0), ("fold", 0, 0)] + [("turn", w, g) for w in range(2) for g in range(2)]
                 + [("M", 0, g) for g in range(4)] + [("turn", 2, g) for g in range(2)] + [("N", 2, g) for g in range(4)])

        def setup_wait_copied(eng, k):
            eng.wait_ge((setup_dve, setup_act)[k % 2], k // 2 + 1)

        def setup_copy(k, copy):
            kind, w, g = SETUP[k]
            src = PS[:, k % 8, :]
            if kind == "self":
                copy(wT[:, :, :].rearrange("p a b -> p (a b)"), src[:, 0:3 * P], 1.0)
            elif kind == "fold":
                copy(wvo[:, :, :].rearrange("p a b -> p (a b)"), src[:, 0:2 * P], 1.0)
            elif kind == "turn":
                copy(wheadsT[:, w, 4 * g:4 * g + 4, :].rearrange("p a b -> p (a b)"), src, 1.0)
            else:
                dst = (MT if kind == "M" else NN)[:, :, :].rearrange("p (b i a) d -> p b a i d", a=2, i=4)
                copy(dst[:, g // 2, g % 2, :, :], src.rearrange("p (i d) -> p i d", d=P),
                     CROSS_SCALE if kind == "M" else 1.0)

        block = ctx.enter_context(nc.Block())

        @block.sync
        def _(sp):
            for k, w in enumerate((Wq, Wk, Wv, Wo)):
                sp.dma_start(wself[:, k, :], w).then_inc(self_in, 16)
            for k, w in enumerate((W_Q, W_K)):
                sp.dma_start(wheads[:, k, :].rearrange("m (h k) -> m h k", h=HEADS),
                             w.rearrange("h m k -> m h k")).then_inc(heads_in[k], 16)
            sp.dma_start(xin[0][:, :, :], x_pairs[0]).then_inc(x_in[0], 16)
            sp.dma_start(cin[0][:, :, :], c_pairs[0]).then_inc(c_in[0], 16)
            sp.dma_start(wheads[:, 2, :].rearrange("m (h k) -> m h k", h=HEADS),
                         W_V.rearrange("h m k -> m h k")).then_inc(heads_in[2], 16)
            sp.dma_start(won[:, :, :], W_O.rearrange("(c p) o -> p c o", p=P)).then_inc(wo_in, 16)

            def load(step, parity, q):
                if not (isinstance(q, int) and q < 2):
                    for name in ("xT", "cT"):
                        wait_apart(sp, full[bank_of(name)], fills_before(step - 1, name) + 1, passed_sp)
                    wait_apart(sp, xbo_done, step + 2, passed_sp)
                sp.dma_start(xin[1 - parity][:, :, :], x_pairs[q]).then_inc(x_in[1 - parity], 16)
                sp.dma_start(cin[1 - parity][:, :, :], c_pairs[q]).then_inc(c_in[1 - parity], 16)

            def store(q, parity):
                wait_apart(sp, x2_done, 2 * q + 2, passed_sp)
                rows = 2 * P
                tab = table.rearrange("(q e t) d -> q t e d", e=2, t=P)
                sm = total.rearrange("(q e t) d -> q t e d", e=2, t=P)
                sp.dma_start(tab[q, :, :, 0:P], x2[parity][:, :, :]).then_inc(stored[parity], 16)
                sp.dma_start(sm[q], x2[parity][:, :, :]).then_inc(stored[parity], 16)

            def step(p, parity, nth, ahead, prep, cross, post):
                if not isinstance(p, int) or p + 3 < PAIRS:
                    load(p, parity, p + 3)
                if post:
                    store(p - 1, 1 - parity)

            attention_steps(sp, step)
            for k in range(2):
                sp.wait_ge(stored[k], 32 * PAIRS // 2)
            sp.wait_ge(gates_done, 1)
            sp.dma_start(table.rearrange("(b t) d -> t b d", t=P)[:, :, P:ROW], gates[:, :, :]).then_inc(gates_stored, 16)
            sp.wait_ge(scattered, 16 * SB * E)
            rows = total.rearrange("(b t) d -> t b d", t=P)
            for c in range(B // 4):
                sp.dma_start(fin[:, 4 * c:4 * c + 4, :], rows[:, 4 * c:4 * c + 4, :]).then_inc(fin_in[c], 16)
            for c in range(B // 4):
                sp.wait_ge(fin_done, 4 * (c + 1))
                sp.dma_start(out.rearrange("b t d -> t b d")[:, 4 * c:4 * c + 4, :],
                             fin[:, 4 * c:4 * c + 4, :]).then_inc(out_done, 16)
            sp.wait_ge(gates_stored, 16)
            sp.wait_ge(out_done, 16 * (B // 4))

        @block.gpsimd
        def _(pool):
            pool.memset(ident[:, :], 0.0).then_inc(consts, 1)
            pool.memset(ones[:, :], 1.0).then_inc(consts, 1)
            pool.wait_ge(consts, 1)
            pool.affine_select(out=ident[:, :], in_=ident[:, :], compare_op=ALU.not_equal, fill=1.0,
                               base=0, pattern=[[-1, P]], channel_multiplier=1).then_inc(consts, 1)
            pool.memset(mhalf[:, :], -0.5).then_inc(consts, 1)
            pool.memset(VOT[:, :, HK:HKP], 0.0).then_inc(consts, 1)
            pool.memset(pn[:, :, HK:HKP], 0.0).then_inc(consts, 1)
            pool.iota(iota[:, :], [[1, P]], base=0, channel_multiplier=0).then_inc(consts, 1)
            pool.iota(iotab[:, :], [[P, B]], base=0, channel_multiplier=0).then_inc(consts, 1)
            pool.iota(iotap[:, :], [[1, 1]], base=0, channel_multiplier=1).then_inc(consts, 1)
            pool.memset(three[:, 3:4], 0).then_inc(consts, 1)
            pool.iota(three[:, 0:3], [[1, 3]], base=1, channel_multiplier=0).then_inc(consts, 1)
            pool.iota(shifts[:, 0:LEFTS], [[-2, LEFTS]], base=answer_shift(0), channel_multiplier=0).then_inc(consts, 1)
            pool.iota(shifts[:, LEFTS:ROUNDS], [[2, ROUNDS - LEFTS]], base=-answer_shift(LEFTS),
                      channel_multiplier=0).then_inc(consts, 1)
            pool.memset(count[:, :, 3:7], float(TOPK)).then_inc(consts, 1)
            pool.memset(groupf[:, :], 0.0).then_inc(consts, 1)
            pool.memset(beforef[:, :], 0.0).then_inc(consts, 1)
            pool.memset(keep[:, :, :], 1.0).then_inc(consts, 1)
            pool.memset(onesb[:, :], 1.0).then_inc(consts, 1)
            pool.wait_ge(consts, 18)
            pool.memset(keep[:, :, 0:1], 0.0).then_inc(consts, 1)
            v = groupf[:, :].rearrange("p (a e) -> p a e", e=E)
            for n in range(-(P // E) + 1, P // E):
                pool.affine_select(out=v, in_=v, compare_op=ALU.not_equal, fill=1.0, base=E * n,
                                   pattern=[[-E, P // E], [-1, E]], channel_multiplier=1).then_inc(consts, 1)
                pool.wait_ge(consts, 19 + n + P // E)
            pool.affine_select(out=beforef[:, :], in_=beforef[:, :], compare_op=ALU.is_gt, fill=-1.0, base=0,
                               pattern=[[1, P]], channel_multiplier=-1).then_inc(consts, 1)
            pool.tensor_copy(pcol[:, :], iotap[:, :]).then_inc(consts, 1)
            pool.wait_ge(consts, CONSTS - 1)
            pool.tensor_copy(before[:, :], beforef[:, :]).then_inc(consts, 1)
            pool.dma_start(w1[:, :, :], W1.rearrange("e d f -> d e f")).then_inc(moe_in, 16)
            pool.dma_start(w2[:, :, :, :].rearrange("p e c d -> p (e c) d"),
                           W2.rearrange("e (c p) d -> p (e c) d", p=P)).then_inc(moe_in, 16)
            pool.wait_ge(setup_act, 1)

            def step(p, parity, nth, ahead, prep, cross, post):
                if prep:
                    wait(pool, x_in[1 - parity], 16 * (nth + 1))
                    for e in range(2):
                        i = pool.tensor_tensor(xbo[:, e, :], xin[1 - parity][:, e, :], wvo[:, 1, :], ALU.add)
                    i.then_inc(xbo_done, 1)
                if cross:
                    for e in range(2):
                        wait(pool, crcp_done, 2 * p + e + 1)
                        pool.tensor_tensor(
                            pn[:, e, 0:HK].rearrange("p (h k) -> p h k", h=HEADS),
                            pc[:, e, :].rearrange("p (h k) -> p h k", h=HEADS),
                            crcp[:, e, :].unsqueeze(2).to_broadcast([P, HEADS, KEYS]),
                            ALU.mult).then_inc(pn_done, 1)
                if prep:
                    wait(pool, var1, p + 2)
                    pool.tensor_tensor(rs1[:, :], ve1[:, :], mhalf[:, :], ALU.pow).then_inc(rstd1, 1)
                if cross:
                    for e in range(2):
                        wait(pool, var2, 2 * p + e + 1)
                        pool.tensor_tensor(rs2[:, e:e + 1], ve2[:, e:e + 1], mhalf[:, 0:1], ALU.pow).then_inc(rstd2, 1)

            attention_steps(pool, step)

            def gather(e):
                pool.wait_ge(idx_done, e + 1)
                if e == 0:
                    pool.wait_ge(gates_stored, 16)
                    for k in range(2):
                        pool.wait_ge(stored[k], 32 * PAIRS // 2)
                if e >= 3:
                    pool.wait_ge(ye_done, 2 * (e - 2))
                for h in range(SB):
                    pool.indirect_dma_start(xg[:, e % 3, h, :], None, table,
                                            bass.IndirectOffsetOnAxis(ap=idx[:, e, h:h + 1], axis=0)
                                            ).then_inc(gathered[e % 3][h], 16)

            def scatter(e):
                if e:
                    pool.wait_ge(scattered, 16 * SB * e)
                for h in range(SB):
                    pool.wait_ge(ye_done, 2 * e + 1 + h // 4)
                    pool.indirect_dma_start(total, bass.IndirectOffsetOnAxis(ap=idx[:, e, h:h + 1], axis=0),
                                            ye[:, e % 2, h, :], None, compute_op=ALU.add).then_inc(scattered, 16)

            gather(0)
            gather(1)
            for e in range(E):
                if e + 2 < E:
                    gather(e + 2)
                scatter(e)
            for c in range(B // 4):
                pool.wait_ge(fin_var, c + 1)
                pool.tensor_tensor(rsf[:, 4 * c:4 * c + 4], vef[:, 4 * c:4 * c + 4],
                                   mhalf[:, 0:1].to_broadcast([P, 4]), ALU.pow).then_inc(fin_rstd, 1)

        @block.scalar
        def _(act):
            act.dma_start(brow[:, 0:P], bo.rearrange("(a n) -> a n", a=1)).then_inc(small_in, 16)
            for k, b in enumerate((bq, bk, bv)):
                act.dma_start(bcol[:, k:k + 1], b.rearrange("(n a) -> n a", a=1)).then_inc(small_in, 16)
            act.dma_start(wr[:, :], Wr).then_inc(route_in, 16)
            act.dma_start(b1n[:, :], b1.rearrange("e (c f) -> (e c) f", f=P)).then_inc(route_in, 16)
            act.dma_start(brow[:, P:P + E * P], b2.rearrange("(a e) d -> a (e d)", a=1)).then_inc(route_in, 16)
            for k in range(1, len(SETUP), 2):
                act.wait_ge(setup_full, k + 1)
                setup_copy(k, lambda dst, src, s: act.activation(dst, src, ACT.Copy, scale=s).then_inc(setup_act, 1))

            def copy(p, name, dst, src):
                ring_wait_full(act, p, name)
                act.activation(dst, src, ACT.Copy).then_inc(free[bank_of(name)], 1)

            def step(p, parity, nth, ahead, prep, cross, post):
                def heads_copy(what, u):
                    name = (what, u)
                    dst = A[1 - parity] if what == "A" else VOT
                    n = len(heads_of(u))
                    copy(p, name, dst[:, :, 3 * u * KEYS:(3 * u + n) * KEYS].rearrange("p e (h k) -> p h e k", h=n),
                         ring[bank_of(name)][:, 0:2 * n * KEYS].rearrange("p (h e k) -> p h e k", h=n, e=2))

                def cross_exp(e):
                    wait(act, s2_free, 2 * p + e + 1)
                    act.activation(pc[:, e, :], pc[:, e, :], ACT.Exp).then_inc(cexp_done, 1)

                def cross_pT(e):
                    for g, (a, b) in enumerate(GROUPS):
                        name = ("P2T", e, g)
                        copy(p, name, pT[:, e, a * P:b * P], ring[bank_of(name)][:, 0:(b - a) * P])

                if prep:
                    ring_wait_full(act, p, "QK")
                    qk = ring[bank_of("QK")]
                    act.activation(qT[:, :, :].rearrange("p e t -> p (e t)"), qk[:, 0:2 * P], ACT.Identity,
                                   bias=bcol[:, 0:1])
                    act.activation(kT[:, :, :].rearrange("p e t -> p (e t)"), qk[:, 2 * P:4 * P], ACT.Identity,
                                   bias=bcol[:, 1:2]).then_inc(free[bank_of("QK")], 1)
                    copy(p, "V", vs[:, :, :].rearrange("p e t -> p (e t)"), ring[bank_of("V")][:, 0:2 * P])
                    heads_copy("A", 0)
                    heads_copy("A", 1)
                if cross:
                    cross_exp(0)
                if prep:
                    heads_copy("A", 2)
                    heads_copy("A", 3)
                    heads_copy("A", 4)
                    wait(act, snb_done, p + 2)
                    for e in range(2):
                        act.activation(pself[:, e, :], small[:, e * P:(e + 1) * P], ACT.Exp, bias=snb[:, e:e + 1],
                                       scale=SELF_SCALE, accum_out=ssum[:, e:e + 1]).then_inc(sexp_done, 1)
                    heads_copy("A", 5)
                    heads_copy("VOT", 0)
                    heads_copy("VOT", 1)
                if cross:
                    cross_exp(1)
                if prep:
                    wait(act, self_full, 4 * (p + 1) + 2)
                    act.activation(pselfT[:, :, :].rearrange("p e t -> p (e t)"), small[:, 0:2 * P],
                                   ACT.Copy).then_inc(self_free, 1)
                if cross:
                    cross_pT(0)
                if prep:
                    for u in range(3, 6):
                        heads_copy("VOT", u)
                if ahead:
                    copy(p, "xT", xT[:, :, :].rearrange("p e t -> p (e t)"), ring[bank_of("xT")][:, 0:2 * P])
                    copy(p, "cT", cT[:, :], ring[bank_of("cT")][:, 0:2 * KEYS])
                if cross:
                    cross_pT(1)
                if prep:
                    wait(act, self_full, 4 * (p + 1) + 4)
                    act.activation(x1T[:, :, :].rearrange("p e t -> p (e t)"), small[:, 0:2 * P],
                                   ACT.Copy).then_inc(self_free, 1)

            act.wait_ge(small_in, 16 * 4)
            attention_steps(act, step)

            act.wait_ge(g_sub, 1)
            act.activation(gates[:, :, :], gates[:, :, :], ACT.Exp).then_inc(g_exp, 1)
            act.wait_ge(late_full, 1)
            act.activation(b1T[:, :], PS[:, 4, 0:E * FC], ACT.Copy).then_inc(late_done, 1)
            act.activation(group[:, :], PS[:, 4, P:2 * P], ACT.Copy).then_inc(late_done, 1)
            act.activation(b2b[:, :, :].rearrange("p (a b) d -> p a (b d)", a=2), PS[:, 5:7, :],
                           ACT.Copy).then_inc(late_done, 1)

            def copy_rows(e, h):
                act.wait_ge(xeT_full, 2 * e + h + 1)
                act.activation(xeT[:, 512 * h:512 * h + 512], PS[:, 3 + h, :], ACT.Copy).then_inc(xeT_done, 1)

            for e in range(E):
                copy_rows(e, 0)
                if e:
                    copy_rows(e, 1)
                for n in range(2 * FC):
                    h, c = divmod(n, FC)
                    if e == 0 and n == FC:
                        copy_rows(0, 1)
                    act.wait_ge(hid_full, 2 * FC * e + n + 1)
                    act.activation(hid[:, c, 512 * h:512 * h + 512], PS[:, HID_BANKS[(2 * FC * e + n) % 3], :], ACT.Gelu,
                                   bias=b1T[:, FC * e + c:FC * e + c + 1]).then_inc(hid_done, 1)

            for c in range(B // 4):
                act.wait_ge(fin_shifted, c + 1)
                for b in range(4 * c, 4 * c + 4):
                    act.activation(fin[:, b, :], fin[:, b, :], ACT.Identity, bias=nmf[:, b:b + 1],
                                   scale=rsf[:, b:b + 1]).then_inc(fin_done, 1)

        @block.vector
        def _(dve):
            for k in range(0, len(SETUP), 2):
                dve.wait_ge(setup_full, k + 1)
                setup_copy(k, lambda dst, src, s: dve.tensor_scalar(dst, src, s, None, ALU.mult).then_inc(setup_dve, 1))

            def step(p, parity, nth, ahead, prep, cross, post):
                def second_norm(q, e, par, earlier):
                    wait(dve, rstd2, 2 * q + e + 1)
                    wait(dve, stored[par], 32 * earlier)
                    dve.tensor_scalar(x2[par][:, e, :], r2[:, e, :], mv2[:, e, 0:1], rs2[:, e:e + 1],
                                      ALU.subtract, ALU.mult).then_inc(x2_done, 1)

                def cross_max(e):
                    wait(dve, s2_full, 2 * p + e + 1)
                    s = PS[:, 0:3, :].rearrange("p a b -> p (a b)")[:, 0:HK].rearrange("p (h k) -> p h k", h=HEADS)
                    dve.tensor_reduce(cmax[:, e, :], s, AX.X, ALU.max).then_inc(cmax_done, 1)

                def cross_sub(e):
                    wait(dve, cmax_done, 2 * p + e + 1)
                    s = PS[:, 0:3, :].rearrange("p a b -> p (a b)")[:, 0:HK].rearrange("p (h k) -> p h k", h=HEADS)
                    dve.tensor_tensor(pc[:, e, :].rearrange("p (h k) -> p h k", h=HEADS), s,
                                      cmax[:, e, :].unsqueeze(2).to_broadcast([P, HEADS, KEYS]),
                                      ALU.subtract).then_inc(s2_free, 1)

                def cross_sum(e):
                    wait(dve, cexp_done, 2 * p + e + 1)
                    dve.tensor_reduce(csum[:, e, :], pc[:, e, :].rearrange("p (h k) -> p h k", h=HEADS), AX.X,
                                      ALU.add).then_inc(csum_done, 1)
                    wait(dve, csum_done, 2 * p + e + 1)
                    dve.reciprocal(crcp[:, e, :], csum[:, e, :]).then_inc(crcp_done, 1)

                def second_stats(e):
                    name = ("AV2", e)
                    ring_wait_full(dve, p, name)
                    dve.tensor_tensor(r2[:, e, :], ring[bank_of(name)][:, 0:P], x1[parity][:, e, :],
                                      ALU.add).then_inc(free[bank_of(name)], 1)
                    ring_wait_copied(dve, p, name)
                    dve.bn_stats(st2[:, e, :], r2[:, e, :]).then_inc(ln2_steps, 1)
                    wait_apart(dve, ln2_steps, 4 * p + 2 * e + 1, passed_dve)
                    dve.bn_aggr(mv2[:, e, :], st2[:, e, :]).then_inc(ln2_steps, 1)
                    wait(dve, ln2_steps, 4 * p + 2 * e + 2)
                    dve.tensor_scalar(ve2[:, e:e + 1], mv2[:, e, 1:2], EPS, None, ALU.add).then_inc(var2, 1)

                def first_norm():
                    wait(dve, sexp_done, 2 * (p + 1) + 2)
                    dve.reciprocal(srcp[:, :], ssum[:, :]).then_inc(srcp_done, 1)
                    wait(dve, srcp_done, p + 2)
                    wait(dve, xbo_done, p + 2)
                    wait(dve, self_full, 4 * (p + 1) + 3)
                    for e in range(2):
                        i = dve.scalar_tensor_tensor(out=r1[:, e, :], in0=small[:, e * P:(e + 1) * P],
                                                     scalar=srcp[:, e:e + 1], in1=xbo[:, e, :],
                                                     op0=ALU.mult, op1=ALU.add)
                    i.then_inc(self_free, 1)
                    wait(dve, self_free, 3 * (p + 1) + 2)
                    for e in range(2):
                        i = dve.bn_stats(st1[:, e, :], r1[:, e, :])
                    i.then_inc(ln1_steps, 1)
                    wait_apart(dve, ln1_steps, 2 * (p + 1) + 1, passed_dve)
                    for e in range(2):
                        i = dve.bn_aggr(mv1[:, e, :], st1[:, e, :])
                    i.then_inc(ln1_steps, 1)
                    wait(dve, ln1_steps, 2 * (p + 1) + 2)
                    dve.tensor_scalar(ve1[:, :], mv1[:, :, 1:2].rearrange("p e a -> p (e a)"), EPS, None,
                                      ALU.add).then_inc(var1, 1)

                def vo_copy(e, g):
                    name = ("VO", e, g)
                    a, b = GROUPS[g]
                    ring_wait_full(dve, p, name)
                    dve.tensor_copy(VO[:, e, a:b, :].rearrange("p c d -> p (c d)"),
                                    ring[bank_of(name)][:, 0:(b - a) * P]).then_inc(free[bank_of(name)], 1)

                if post:
                    second_norm(p - 1, 1, 1 - parity, nth - 1)
                if cross:
                    cross_max(0)
                    cross_sub(0)
                if post:
                    ring_wait_full(dve, p, "x2T")
                    dve.tensor_copy(x2T[:, :, :].rearrange("p e t -> p (e t)"),
                                    ring[bank_of("x2T")][:, 0:2 * P]).then_inc(free[bank_of("x2T")], 1)
                if cross:
                    cross_sum(0)
                    cross_max(1)
                if prep:
                    wait(dve, self_full, 4 * (p + 1) + 1)
                    dve.tensor_reduce(smax[:, :], small[:, 0:2 * P].rearrange("p (e k) -> p e k", e=2), AX.X,
                                      ALU.max).then_inc(smax_done, 1)
                    wait(dve, smax_done, p + 2)
                    dve.tensor_scalar(snb[:, :], smax[:, :], -SELF_SCALE, None, ALU.mult).then_inc(snb_done, 1)
                if post:
                    ring_wait_full(dve, p, "LG")
                    dve.tensor_copy(logits[:, bass.ds(2 * (p - 1), 2), :].rearrange("p e n -> p (e n)"),
                                    ring[bank_of("LG")][:, 0:2 * E]).then_inc(free[bank_of("LG")], 1)
                if cross:
                    cross_sub(1)
                if prep:
                    u = 2
                    name = ("VOT", u)
                    n = len(heads_of(u))
                    ring_wait_full(dve, p, name)
                    dve.tensor_copy(VOT[:, :, 3 * u * KEYS:(3 * u + n) * KEYS].rearrange("p e (h k) -> p h e k", h=n),
                                    ring[bank_of(name)][:, 0:2 * n * KEYS].rearrange("p (h e k) -> p h e k", h=n, e=2)
                                    ).then_inc(free[bank_of(name)], 1)
                if cross:
                    cross_sum(1)
                if prep:
                    first_norm()
                if prep:
                    wait(dve, rstd1, p + 2)
                    for e in range(2):
                        dve.tensor_scalar(x1[1 - parity][:, e, :], r1[:, e, :], mv1[:, e, 0:1], rs1[:, e:e + 1],
                                          ALU.subtract, ALU.mult).then_inc(x1_done, 1)
                if cross:
                    second_stats(0)
                if prep:
                    for g in range(3):
                        vo_copy(0, g)
                if cross:
                    second_norm(p, 0, parity, nth - parity)
                    second_stats(1)
                if prep:
                    for g in range(3):
                        vo_copy(1, g)

            dve.wait_ge(consts, CONSTS)
            for r in range(ROUNDS + 1):
                shift = max(2 * (ROUNDS - 1 - r), 0)
                if r == 0:
                    i = dve.tensor_scalar(pattern[:, r, :], three[:, :], shift, None, ALU.logical_shift_left)
                elif r < ROUNDS:
                    i = dve.tensor_scalar(pattern[:, r, :], three[:, :], shift, shifted_four(r - 1),
                                          ALU.logical_shift_left, ALU.bitwise_xor)
                else:
                    i = dve.tensor_scalar(pattern[:, r, :], three[:, :], 0, shifted_four(r - 1),
                                          ALU.bitwise_and, ALU.bitwise_xor)
            i.then_inc(chain, 1)

            attention_steps(dve, step)
            links = [1]

            def link(i):
                links[0] += 1
                i.then_inc(chain, 1)
                dve.wait_ge(chain, links[0])

            ring_wait_copied(dve, PAIRS, "LG")
            link(dve.tensor_reduce(gmax[:, :], logits[:, :, :], AX.X, ALU.max))
            dve.tensor_tensor(gates[:, :, :], logits[:, :, :], gmax[:, :].unsqueeze(2).to_broadcast([P, B, E]),
                              ALU.subtract).then_inc(g_sub, 1)
            dve.wait_ge(g_exp, 1)
            link(dve.tensor_reduce(gsum[:, :], gates[:, :, :], AX.X, ALU.add))
            link(dve.reciprocal(grcp[:, :], gsum[:, :]))
            dve.tensor_tensor(gates[:, :, :], gates[:, :, :], grcp[:, :].unsqueeze(2).to_broadcast([P, B, E]),
                              ALU.mult).then_inc(gates_done, 1)
            dve.wait_ge(gatesT_full, 1)
            link(dve.tensor_copy(gatesT[:, :], PS[:, 0, 0:2 * P]))

            for r in range(ROUNDS):
                now = pattern[:, 0, :] if r == 0 else cand[:, r % 2, :]
                for j in range(3):
                    i = dve.tensor_scalar(above[:, j, :], gatesT[:, :], now[:, j:j + 1].bitcast(F32), None,
                                          ALU.is_ge, ALU.add, accum_out=count[:, r % 2, j:j + 1])
                i.then_inc(counted, 1)
                dve.tensor_tensor(nextpat[:, :], pattern[:, r + 1, :], now[:, 3:4].to_broadcast([P, 4]),
                                  ALU.bitwise_xor)
                dve.wait_ge(summed, r + 1)
                link(dve.tensor_scalar(passed[:, :], PS[:, 1, 0:7], float(TOPK), None, ALU.is_ge, ALU.add,
                                       accum_out=npassed[:, :]))
                link(dve.scalar_tensor_tensor(
                    out=cand[:, (r + 1) % 2, :], in0=npassed[:, :].bitcast(I32).to_broadcast([P, 4]),
                    scalar=shifts[:, r:r + 1], in1=nextpat[:, :],
                    op0=ALU.logical_shift_left if r < LEFTS else ALU.logical_shift_right, op1=ALU.bitwise_xor))
            dve.tensor_scalar(thr8[:, :], ident[0:E, 0:E], cand[0:E, ROUNDS % 2, 3:4].bitcast(F32), None,
                              ALU.mult).then_inc(thr8_done, 1)
            dve.wait_ge(thrb_full, 1)
            link(dve.tensor_copy(thrb[:, :], PS[:, 1, 8:8 + E]))
            g = gates[:, :, :].rearrange("p b e -> p e b")
            t = thrb[:, :].unsqueeze(2).to_broadcast([P, E, B])
            dve.tensor_tensor(taken[:, :, 0, :], g, t, ALU.is_gt)
            dve.tensor_tensor(taken[:, :, 1, :], g, t, ALU.is_equal).then_inc(taken_done, 1)
            dve.wait_ge(prefix_full, 1)
            flat = "p e a b -> p (e a b)"
            link(dve.tensor_tensor_scan(totals[:, :], keep[:, :, :].rearrange("p n b -> p (n b)"), PS[:, 3, :], 0.0,
                                        ALU.mult, ALU.add))
            link(dve.tensor_tensor(slot2[:, :, :, :].rearrange(flat), PS[:, 2, :], totals[:, :], ALU.add))
            link(dve.scalar_tensor_tensor(out=slot[:, :, :, :].rearrange(flat), in0=slot2[:, :, :, :].rearrange(flat),
                                          scalar=-NONE, in1=taken[:, :, :, :].rearrange(flat), op0=ALU.add, op1=ALU.mult))
            link(dve.scalar_tensor_tensor(out=sloti[:, :, :], in0=slot[:, :, 0, :], scalar=NONE, in1=slot[:, :, 1, :],
                                          op0=ALU.add, op1=ALU.add))
            dve.tensor_scalar(slotlo[:, :, :], sloti[:, :, :], P - 1, None, ALU.bitwise_and)
            link(dve.tensor_scalar(slothi[:, :, :], sloti[:, :, :], 7, None, ALU.logical_shift_right))

            def one_hots(e):
                if e:
                    dve.wait_ge(list_full, e)
                link(dve.tensor_tensor(hot8[:, :, :], slothi[:, e, :].unsqueeze(2).to_broadcast([P, B, SB]),
                                       iota[:, 0:SB].unsqueeze(1).to_broadcast([P, B, SB]), ALU.is_equal))
                dve.tensor_tensor(tokens[:, :, :, 0], hot8[:, :, :],
                                  iotab[:, :].unsqueeze(2).to_broadcast([P, B, SB]), ALU.mult)
                dve.tensor_scalar(tokens[:, :, :, 1], hot8[:, :, :], pcol[:, 0:1], None, ALU.mult).then_inc(tokens_done, 1)
                for q in range(4):
                    b = B // 4 * q
                    dve.tensor_tensor(onehot[:, b:b + B // 4, :], iota[:, :].unsqueeze(1).to_broadcast([P, B // 4, P]),
                                      slotlo[:, e, b:b + B // 4].unsqueeze(2).to_broadcast([P, B // 4, P]),
                                      ALU.is_equal).then_inc(onehot_done, 1)

            def make_idx(e):
                dve.wait_ge(list_full, e + 1)
                with nc.allow_low_precision(reason="numbers of tokens are whole and below 2 ** 24"):
                    dve.tensor_reduce(idx[:, e, :], PS[:, 7, 0:2 * SB].rearrange("p (s a) -> p s a", a=2), AX.X,
                                      ALU.add).then_inc(idx_done, 1)

            def results(e, h):
                if e >= 2:
                    dve.wait_ge(scattered, 16 * SB * (e - 1))
                dve.wait_ge(ye_full, 2 * e + h + 1)
                dve.tensor_tensor(yb[:, 4 * h:4 * h + 4, :], PS[:, 1 + h, :].rearrange("p (s d) -> p s d", d=P),
                                  b2b[:, e:e + 1, :].to_broadcast([P, 4, P]), ALU.add).then_inc(ye_added, 1)
                dve.wait_ge(ye_added, 2 * e + h + 1)
                for s in range(4 * h, 4 * h + 4):
                    dve.wait_ge(gathered[e % 3][s], 16 * (e // 3 + 1))
                dve.tensor_tensor(ye[:, e % 2, 4 * h:4 * h + 4, :], yb[:, 4 * h:4 * h + 4, :],
                                  xg[:, e % 3, 4 * h:4 * h + 4, P + e:P + e + 1].to_broadcast([P, 4, P]),
                                  ALU.mult).then_inc(ye_done, 1)

            for e in range(3):
                one_hots(e)
                make_idx(e)
            for e in range(E):
                if e + 3 < E:
                    one_hots(e + 3)
                results(e, 0)
                if e + 3 < E:
                    make_idx(e + 3)
                results(e, 1)

            def fin_shift(c):
                dve.wait_ge(fin_rstd, c + 1)
                dve.scalar_tensor_tensor(out=nmf[:, 4 * c:4 * c + 4],
                                         in0=mvf[:, 4 * c:4 * c + 4, 0:1].rearrange("p b a -> p (b a)"), scalar=-1.0,
                                         in1=rsf[:, 4 * c:4 * c + 4], op0=ALU.mult, op1=ALU.mult).then_inc(fin_shifted, 1)

            for c in range(B // 4):
                dve.wait_ge(fin_in[c], 16)
                for b in range(4 * c, 4 * c + 4):
                    i = dve.bn_stats(stf[:, b, :], fin[:, b, :])
                link(i)
                for b in range(4 * c, 4 * c + 4):
                    i = dve.bn_aggr(mvf[:, b, :], stf[:, b, :])
                link(i)
                dve.tensor_scalar(vef[:, 4 * c:4 * c + 4], mvf[:, 4 * c:4 * c + 4, 1:2].rearrange("p b a -> p (b a)"), EPS,
                                  None, ALU.add).then_inc(fin_var, 1)
                if c:
                    fin_shift(c - 1)
            fin_shift(B // 4 - 1)

        @block.tensor
        def _(pe):
            pe.wait_ge(consts, 2)

            def keep_warm(n):
                for _ in range(n):
                    pe.matmul(PS[:, 7, 0:P], ones[:, :], ones[:, :], start=True, stop=True)

            keep_warm(WARM["start"])
            pe.wait_ge(consts, 4)
            for k, (kind, w, g) in enumerate(SETUP):
                if k >= 8:
                    setup_wait_copied(pe, k - 8)
                bank = PS[:, k % 8, :]
                if kind == "self":
                    pe.wait_ge(self_in, 16 * 4)
                    for j, n in enumerate((0, 1, 3)):
                        i = pe.transpose(bank[:, j * P:(j + 1) * P], wself[:, n, :], ident[:, :])
                elif kind == "fold":
                    pe.wait_ge(small_in, 16 * 4)
                    setup_wait_copied(pe, 0)
                    pe.matmul(bank[:, 0:P], wself[:, 2, :], wT[:, 2, :], start=True, stop=True)
                    pe.matmul(bank[:, P:2 * P], bcol[:, 2:3].to_broadcast([P, P]), wT[:, 2, :], start=True, stop=False)
                    i = pe.matmul(bank[:, P:2 * P], ones[0:1, :], brow[0:1, 0:P], start=False, stop=True)
                elif kind == "turn":
                    if g == 0:
                        pe.wait_ge(heads_in[w], 16)
                    for j in range(4):
                        c = 4 * g + j
                        i = pe.transpose(bank[:, j * P:(j + 1) * P], wheads[:, w, c * P:(c + 1) * P], ident[:, :])
                else:
                    setup_wait_copied(pe, SETUP.index(("turn", 1 if kind == "M" else 2, g // 2)))
                    if kind == "N" and g == 0:
                        pe.wait_ge(wo_in, 16)
                    lo = DK * (g % 2)
                    for j in range(4):
                        c = 4 * (g // 2) + j
                        lhsT = wheadsT[lo:lo + DK, 1 if kind == "M" else 2, c, :]
                        rhs = wheadsT[lo:lo + DK, 0, c, :] if kind == "M" else won[lo:lo + DK, c, :]
                        i = pe.matmul(bank[:, j * P:(j + 1) * P], lhsT, rhs, start=True, stop=True)
                i.then_inc(setup_full, 1)
                keep_warm(WARM.get(SETUP[k], 0))
            setup_wait_copied(pe, len(SETUP) - 2)
            setup_wait_copied(pe, len(SETUP) - 1)
            pe.wait_ge(consts, 6)
            pe.wait_ge(route_in, 16 * 3)

            def step(p, parity, nth, ahead, prep, cross, post):
                def unit(name):
                    ring_wait_free(pe, p, name)
                    return ring[bank_of(name)]

                def done(i, name):
                    i.then_inc(full[bank_of(name)], 1)

                def heads(what, u):
                    name = (what, u)
                    bank = unit(name)
                    w = MT if what == "A" else NN
                    for j, h in enumerate(heads_of(u)):
                        i = pe.matmul(bank[:, j * 2 * KEYS:(j + 1) * 2 * KEYS], w[:, h, :], cT[:, :],
                                      start=True, stop=True)
                    done(i, name)

                def cross_scores(e):
                    wait(pe, s2_free, 2 * p + e)
                    for n in range(3):
                        a, b = n * 512, min((n + 1) * 512, HK)
                        i = pe.matmul(PS[:, n, 0:b - a], x1T[:, e, :], A[parity][:, e, a:b], start=True, stop=True)
                    i.then_inc(s2_full, 1)

                def cross_pT(e):
                    wait(pe, pn_done, 2 * p + e + 1)
                    for g, (a, b) in enumerate(GROUPS):
                        name = ("P2T", e, g)
                        bank = unit(name)
                        for c in range(a, b):
                            i = pe.transpose(bank[:, (c - a) * P:(c - a + 1) * P], pn[:, e, c * P:(c + 1) * P], ident[:, :])
                        done(i, name)

                def cross_out(e):
                    name = ("AV2", e)
                    bank = unit(name)
                    ring_wait_copied(pe, p - 1, ("VO", e, 2))
                    ring_wait_copied(pe, p, ("P2T", e, 2))
                    for c in range(CH):
                        i = pe.matmul(bank[:, 0:P], pT[:, e, c * P:(c + 1) * P], VO[:, e, c, :],
                                      start=(c == 0), stop=(c == CH - 1))
                    done(i, name)

                def vo_transposes(e):
                    for g, (a, b) in enumerate(GROUPS):
                        name = ("VO", e, g)
                        bank = unit(name)
                        for c in range(a, b):
                            i = pe.transpose(bank[:, (c - a) * P:(c - a + 1) * P], VOT[:, e, c * P:(c + 1) * P], ident[:, :])
                        done(i, name)

                alone = isinstance(p, int) and p == PAIRS - 1
                if cross:
                    wait(pe, self_free, 3 * p + 3)
                    cross_scores(0)
                if prep:
                    bank = unit("QK")
                    ring_wait_copied(pe, p - 1, "xT")
                    for j in range(2):
                        i = pe.matmul(bank[:, j * 2 * P:(j + 1) * 2 * P], wT[:, j, :],
                                      xT[:, :, :].rearrange("p e t -> p (e t)"), start=True, stop=True)
                    done(i, "QK")
                    bank = unit("V")
                    for e in range(2):
                        i = pe.matmul(bank[:, e * P:(e + 1) * P], xT[:, e, :], wvo[:, 0, :], start=True, stop=True)
                    done(i, "V")
                    ring_wait_copied(pe, p - 1, "cT")
                    heads("A", 0)
                    heads("A", 1)
                if post:
                    wait(pe, x2_done, 2 * (p - 1) + 2)
                    bank = unit("x2T")
                    for e in range(2):
                        i = pe.transpose(bank[:, e * P:(e + 1) * P], x2[1 - parity][:, e, :], ident[:, :])
                    done(i, "x2T")
                if prep:
                    heads("A", 2)
                if cross:
                    keep_warm(14 if alone else 0)
                    cross_scores(1)
                if prep:
                    wait(pe, self_free, 3 * (p + 1))
                    ring_wait_copied(pe, p, "QK")
                    for e in range(2):
                        i = pe.matmul(small[:, e * P:(e + 1) * P], qT[:, e, :], kT[:, e, :], start=True, stop=True)
                    i.then_inc(self_full, 1)
                    heads("A", 3)
                if post:
                    bank = unit("LG")
                    ring_wait_copied(pe, p, "x2T")
                    for e in range(2):
                        i = pe.matmul(bank[:, e * E:(e + 1) * E], x2T[:, e, :], wr[:, :], start=True, stop=True)
                    done(i, "LG")
                if prep:
                    heads("A", 4)
                    heads("A", 5)
                    heads("VOT", 0)
                    heads("VOT", 1)
                    wait(pe, sexp_done, 2 * (p + 1) + 2)
                    for e in range(2):
                        i = pe.transpose(small[:, e * P:(e + 1) * P], pself[:, e, :], ident[:, :])
                    i.then_inc(self_full, 1)
                    heads("VOT", 2)
                if cross:
                    keep_warm(6 if alone else 0)
                    cross_pT(0)
                if prep:
                    heads("VOT", 3)
                    heads("VOT", 4)
                    wait(pe, self_free, 3 * (p + 1) + 1)
                    for e in range(2):
                        i = pe.matmul(small[:, e * P:(e + 1) * P], pselfT[:, e, :], vs[:, e, :], start=True, stop=True)
                    i.then_inc(self_full, 1)
                    heads("VOT", 5)
                if ahead:
                    count = 16 * (nth + 2 - parity)
                    wait(pe, x_in[parity], count)
                    wait(pe, c_in[parity], count)
                    bank = unit("xT")
                    for e in range(2):
                        i = pe.transpose(bank[:, e * P:(e + 1) * P], xin[parity][:, e, :], ident[:, :])
                    done(i, "xT")
                    bank = unit("cT")
                    for e in range(2):
                        i = pe.transpose(bank[:, e * KEYS:(e + 1) * KEYS], cin[parity][:, e, :], ident[0:KEYS, 0:KEYS])
                    done(i, "cT")
                if cross:
                    keep_warm(10 if alone else 0)
                    cross_out(0)
                    cross_pT(1)
                if prep:
                    ring_wait_copied(pe, p, ("VOT", HEAD_UNITS - 1))
                    vo_transposes(0)
                    wait(pe, x1_done, 2 * (p + 1) + 2)
                    for e in range(2):
                        i = pe.transpose(small[:, e * P:(e + 1) * P], x1[1 - parity][:, e, :], ident[:, :])
                    i.then_inc(self_full, 1)
                if cross:
                    cross_out(1)
                if prep:
                    vo_transposes(1)

            attention_steps(pe, step)

            for k in range(RING_BANKS):
                n = sum(1 for j in range(len(UNITS)) if j % RING_BANKS == k) * PAIRS
                pe.wait_ge(free[k], n)
            pe.wait_ge(gates_done, 1)
            for g in range(2):
                i = pe.transpose(PS[:, 0, g * P:(g + 1) * P],
                                 gates[:, B // 2 * g:B // 2 * (g + 1), :].rearrange("p b e -> p (b e)"), ident[:, :])
            i.then_inc(gatesT_full, 1)
            pe.wait_ge(consts, CONSTS)
            pe.transpose(PS[:, 4, 0:E * FC], b1n[:, :], ident[0:E * FC, 0:E * FC])
            pe.transpose(PS[:, 4, P:2 * P], groupf[:, :], ident[:, :])
            for j in range(2):
                i = pe.matmul(PS[:, 5 + j, :], ones[0:1, :], brow[0:1, P + 512 * j:P + 512 * (j + 1)],
                              start=True, stop=True)
            i.then_inc(late_full, 1)
            pe.wait_ge(late_done, 3)
            for r in range(ROUNDS):
                pe.wait_ge(counted, r + 1)
                pe.matmul(PS[:, 1, 0:7], group[:, :], count[:, r % 2, :], start=True, stop=True).then_inc(summed, 1)
            pe.wait_ge(thr8_done, 1)
            pe.matmul(PS[:, 1, 8:8 + E], ones[0:E, :], thr8[:, :], start=True, stop=True).then_inc(thrb_full, 1)
            pe.wait_ge(taken_done, 1)
            t = taken[:, :, :, :].rearrange("p e a b -> p (e a b)")
            pe.matmul(PS[:, 2, :], before[:, :], t, start=True, stop=True)
            pe.matmul(PS[:, 3, :], onesb[:, :], t, start=True, stop=True).then_inc(prefix_full, 1)

            def make_list(e):
                pe.wait_ge(tokens_done, e + 1)
                if e:
                    pe.wait_ge(idx_done, e)
                for b in range(B):
                    if b % (B // 4) == 0:
                        pe.wait_ge(onehot_done, 4 * e + b // (B // 4) + 1)
                    i = pe.matmul(PS[:, 7, 0:2 * SB], onehot[:, b, :], tokens[:, b, :, :].rearrange("p s a -> p (s a)"),
                                  start=(b == 0), stop=(b == B - 1))
                i.then_inc(list_full, 1)

            def transpose_rows(e, h):
                if e:
                    pe.wait_ge(xeT_done, 2 * (e - 1) + h + 1)
                for s in range(4):
                    pe.wait_ge(gathered[e % 3][4 * h + s], 16 * (e // 3 + 1))
                    i = pe.transpose(PS[:, 3 + h, s * P:(s + 1) * P], xg[:, e % 3, 4 * h + s, 0:P], ident[:, :])
                i.then_inc(xeT_full, 1)

            def hidden(e, h):
                pe.wait_ge(xeT_done, 2 * e + h + 1)
                for c in range(FC):
                    k = 2 * FC * e + FC * h + c
                    if k >= 3:
                        pe.wait_ge(hid_done, k - 2)
                    pe.matmul(PS[:, HID_BANKS[k % 3], :], w1[:, e, c * P:(c + 1) * P], xeT[:, 512 * h:512 * h + 512],
                              start=True, stop=True).then_inc(hid_full, 1)

            def second_layer(e, h):
                pe.wait_ge(hid_done, 2 * FC * e + FC * (h + 1))
                if e:
                    pe.wait_ge(ye_added, 2 * (e - 1) + h + 1)
                for s in range(4):
                    for c in range(FC):
                        i = pe.matmul(PS[:, 1 + h, s * P:(s + 1) * P], hid[:, c, (4 * h + s) * P:(4 * h + s + 1) * P],
                                      w2[:, e, c, :], start=(c == 0), stop=(c == FC - 1))
                i.then_inc(ye_full, 1)

            make_list(0)
            make_list(1)
            pe.wait_ge(moe_in, 32)
            transpose_rows(0, 0)
            for e in range(E):
                hidden(e, 0)
                if e == 0:
                    transpose_rows(0, 1)
                    make_list(2)
                hidden(e, 1)
                second_layer(e, 0)
                if e + 1 < E:
                    transpose_rows(e + 1, 0)
                    transpose_rows(e + 1, 1)
                if e + 3 < E:
                    make_list(e + 3)
                second_layer(e, 1)


_INS = ["x", "ctx_1024", "L0_attn_Wq", "L0_attn_bq", "L0_attn_Wk", "L0_attn_bk", "L0_attn_Wv", "L0_attn_bv",
        "L0_attn_Wo", "L0_attn_bo", "L0_xattn_W_Q", "L0_xattn_W_K", "L0_xattn_W_V", "L0_xattn_W_O",
        "L0_ffn_Wr", "L0_ffn_W1", "L0_ffn_b1", "L0_ffn_W2", "L0_ffn_b2"]


def kernel(**inputs):
    import numpy as _np
    import concourse.bacc as _bacc
    from concourse import mybir as _mybir
    from concourse.bass_utils import run_bass_kernel_spmd as _run

    nc = _bacc.Bacc("TRN2", target_bir_lowering=False, num_devices=1)
    arrays, args = {}, []
    for name in _INS:
        a = _np.ascontiguousarray(inputs[name])
        arrays[f"in_{name}"] = a
        args.append(nc.dram_tensor(f"in_{name}", a.shape, _mybir.dt.from_np(a.dtype), kind="ExternalInput").ap())
    args.append(nc.dram_tensor("out_x", (B, P, P), F32, kind="ExternalOutput").ap())
    decoder_layer(nc, *args)
    r = _run(nc, [arrays], core_ids=[0])
    return r.results[0]["out_x"]
```

```python
from contextlib import ExitStack

import concourse.bass as bass
from concourse import mybir

ALU = mybir.AluOpType
ACT = mybir.ActivationFunctionType
AX = mybir.AxisListType
F32 = mybir.dt.float32
F32R = mybir.dt.float32r
BF16 = mybir.dt.bfloat16
I32 = mybir.dt.int32

P = 128
B = 32
PAIRS = B // 2
KEYS = 77
HEADS = 16
DK = 64
HK = HEADS * KEYS
CH = -(-HK // P)
HKP = CH * P
E = 8
F = 512
FC = F // P
EPS = 1e-5
SELF_SCALE = 1.0 / 8.0
CROSS_SCALE = 1.0 / 8.0
ROW = P + E

RING_BANKS = 4
VOT_UNITS = [(("VOT", h), "ahead") for h in range(HEADS)]
A_UNITS = [(("A", h), "prep") for h in range(HEADS)]
P2T_UNITS = [[(("P2T", e, g), "cross") for g in range(3)] for e in range(2)]
UNITS = [
    [(("VO", 1, 1, g), "prep") for g in range(3)] + [("cT", "ahead"), ("QK", "prep"), ("V", "prep"), ("x2T", "post")]
    + VOT_UNITS[0:12] + P2T_UNITS[0] + VOT_UNITS[12:16] + [(("AV2", 0), "cross")]
    + P2T_UNITS[1] + [("LG", "post"), ("xT", "ahead"), (("AV2", 1), "cross")],
    [("QK", "prep"), ("V", "prep"), ("x2T", "post")] + [(("VO", 0, e, g), "prep") for e in range(2) for g in range(3)]
    + A_UNITS[0:4] + [("LG", "post")] + A_UNITS[4:12] + P2T_UNITS[0] + A_UNITS[12:16]
    + [("xT", "ahead"), (("AV2", 0), "cross")]
    + P2T_UNITS[1] + [(("VO", 1, 0, g), "prep") for g in range(3)] + [(("AV2", 1), "cross")],
]
for units in UNITS:
    while len(units) % RING_BANKS:
        units.append((("none", len(units)), None))
SLOT = [{name: k for k, (name, _) in enumerate(units)} for units in UNITS]
LEAD = {"ahead": 2, "prep": 1, "cross": 0, "post": -1}
BY_DVE = (8, 9, 10, 11)
GROUPS = [(0, 4), (4, 8), (8, CH)]
TOKENS = B * P
TOPK = max(4, -(-2 * TOKENS // E))
SB = TOPK // P
NONE = float(TOKENS)
WARM = {"start": 12, "end": 7, "context": 5, ("fold", 0, 0): 3, ("turn", 0, 1): 10, ("turn", 1, 1): 3}
ROUNDS = 15


FOUR = 0x40800000
NBIT = 21


def answer_shift(r):
    return 2 * (ROUNDS - 1 - r) - NBIT


LEFTS = sum(answer_shift(r) > 0 for r in range(ROUNDS))


def shifted_four(r):
    k = answer_shift(r)
    v = FOUR << k & 0xFFFFFFFF if k >= 0 else FOUR >> -k
    return v - (1 << 32) if v >> 31 else v


def clip(n, most):
    return max(0, min(n, most)) if isinstance(n, int) else n


def bank_of(at, name):
    return SLOT[at[1]][name] % RING_BANKS


def step_before(at):
    p, parity, nth = at
    return p - 1, 1 - parity, nth - parity


def active(step, stage):
    return stage is not None and 0 <= step + LEAD[stage] < PAIRS


def fills_before(at, name):
    p, parity, nth = at
    bank = bank_of(at, name)
    steady = not isinstance(p, int)
    first = 2 - parity if steady else p
    total = sum(active(q, stage) for q in range(-2, first) for k, (_, stage) in enumerate(UNITS[q % 2])
                if k % RING_BANKS == bank)
    total += sum(active(first, stage) for k, (_, stage) in enumerate(UNITS[parity][:SLOT[parity][name]])
                 if k % RING_BANKS == bank)
    if steady:
        each = sum(stage is not None and k % RING_BANKS == bank for units in UNITS for k, (_, stage) in enumerate(units))
        total = each * (nth - 1) + total
    return total


def by_act(c):
    return 2 if c == B // 4 - 1 else 4 - (c % 2 == 0)


def wait(eng, sem, count):
    if isinstance(count, int) and count <= 0:
        return
    eng.wait_ge(sem, count)


def wait_apart(eng, sem, count, passed):
    wait(eng, sem, count)
    if not isinstance(count, int):
        eng.sem_inc(passed, 1)


def attention_steps(eng, step):
    def at(p, parity, nth):
        steady = not isinstance(p, int)
        step(p, parity, nth, steady or p + 2 < PAIRS, steady or -1 <= p < PAIRS - 1, steady or 0 <= p < PAIRS,
             steady or p > 0)

    at(-2, 0, -1)
    at(-1, 1, 0)
    at(0, 0, 0)
    with eng.Fori(0, (PAIRS - 4) // 2) as i:
        at(2 * i + 1, 1, i + 1)
        at(2 * i + 2, 0, i + 1)
    for p in range(PAIRS - 3, PAIRS + 1):
        at(p, p % 2, (p + 1) // 2)


def decoder_layer(nc, x, ctx_1024, Wq, bq, Wk, bk, Wv, bv, Wo, bo, W_Q, W_K, W_V, W_O, Wr, W1, b1, W2, b2, out):
    ctx = ExitStack()
    with ctx:
        def sb(name, shape, dt=F32):
            return ctx.enter_context(nc.sbuf_tensor(name, shape, dt))

        def sem(name):
            return ctx.enter_context(nc.semaphore(name))

        PS = ctx.enter_context(nc.psum_tensor("PS", [P, 8, 512], F32))
        ring = [PS[:, 3 + k, :] for k in range(RING_BANKS)]
        small = PS[:, 7, :]

        ident = sb("ident", [P, P])
        ones = sb("ones", [P, P])
        mhalf = sb("mhalf", [P, 2])
        wself = sb("wself", [P, 4, P])
        brow = sb("brow", [1, P + E * P])
        bcol = sb("bcol", [P, 3])
        shared1 = sb("shared1", [P, 3 * SB * ROW])
        wheads = shared1[:, 0:3 * HEADS * DK].rearrange("p (w n) -> p w n", w=3)
        xg = shared1[:, :].rearrange("p (b s n) -> p b s n", b=3, s=SB)
        won = sb("won", [P, HEADS // 2, P])
        wT = sb("wT", [P, 3, P])
        wvo = sb("wvo", [P, 2, P])
        wheadsT = sb("wheadsT", [P, 3, HEADS // 2, P])
        with ExitStack() as attention:
            def part(name, shape, dt=F32):
                return attention.enter_context(nc.sbuf_tensor(name, shape, dt))

            halves = [part(f"heads_{k}", [P, 2 * HEADS, P], F32R) for k in ("hi", "lo")]
            cT = [part(f"cT_{k}", [P, 4 * KEYS], F32R) for k in ("hi", "lo")]
            VOeven = part("VOeven", [P, 2 * HKP])
        MT = [t[:, 0:HEADS, :] for t in halves]
        NN = [t[:, HEADS:2 * HEADS, :] for t in halves]
        fin = sb("fin", [P, B, P])
        w1 = sb("w1", [P, E, F])
        w2 = sb("w2", [P, E, FC, P])
        wr = sb("wr", [P, E])
        b1n = sb("b1n", [E * FC, P])
        b1T = sb("b1T", [P, E * FC])
        b2b = sb("b2b", [P, E, P])
        xin = [sb(f"xin{k}", [P, 2, P]) for k in range(2)]
        cin = [sb(f"cin{k}", [KEYS, 2, P]) for k in range(2)]
        xbo = sb("xbo", [P, 2, P])
        xT = sb("xT", [P, 2, P])
        qT = sb("qT", [P, 2, P])
        kT = sb("kT", [P, 2, P])
        vs = sb("vs", [P, 2, P])
        smax = sb("smax", [P, 2])
        snb = sb("snb", [P, 2])
        pself = sb("pself", [P, 2, P])
        ssum = sb("ssum", [P, 2])
        srcp = sb("srcp", [P, 2])
        pselfT = sb("pselfT", [P, 2, P])
        r1 = sb("r1", [P, 2, P])
        st1 = sb("st1", [P, 2, 6])
        mv1 = sb("mv1", [P, 2, 2])
        ve1 = sb("ve1", [P, 2])
        rs1 = sb("rs1", [P, 2])
        x1 = [sb(f"x1_{k}", [P, 2, P]) for k in range(2)]
        x1T = sb("x1T", [P, 2, P])
        shared3 = sb("shared3", [P, 4 * HK])
        A = shared3[:, :].rearrange("p (b n) -> p b n", b=4)
        hid = shared3[:, 0:FC * TOPK].rearrange("p (c t) -> p c t", c=FC)
        VOT = sb("VOT", [P, 4, HKP])
        VO = [t.rearrange("p (e c d) -> p e c d", e=2, c=CH)
              for t in (VOeven[:, :], shared1[:, 0:2 * HKP])]
        pc = sb("pc", [P, 2, HK])
        onehot = pc[:, :, :].rearrange("p e n -> p (e n)")[:, 0:B * P // 2].bitcast(BF16).rearrange(
            "p (b s) -> p b s", b=B)
        pn = sb("pn", [P, 2, HKP])
        ye = pn[:, :, :].rearrange("p e n -> p (e n)")[:, 0:2 * TOPK].rearrange("p (b s d) -> p b s d", b=2, s=SB)
        pT = sb("pT", [P, 2, HKP])
        xeT = pT[:, 0, 0:TOPK]
        cmax = sb("cmax", [P, 2, HEADS])
        csum = sb("csum", [P, 2, HEADS])
        crcp = sb("crcp", [P, 2, HEADS])
        r2 = sb("r2", [P, 2, P])
        st2 = sb("st2", [P, 2, 6])
        mv2 = sb("mv2", [P, 2, 2])
        ve2 = sb("ve2", [P, 2])
        rs2 = sb("rs2", [P, 2])
        x2 = [sb(f"x2_{k}", [P, 2, P]) for k in range(2)]
        x2T = sb("x2T", [P, 2, P])
        logits = sb("logits", [P, B, E])
        gates = sb("gates", [P, B, E])
        gmax = sb("gmax", [P, B])
        gsum = sb("gsum", [P, B])
        grcp = sb("grcp", [P, B])
        gatesT = sb("gatesT", [P, 2 * P])
        above = sb("above", [P, 3, 2 * P], BF16)
        count = sb("count", [P, 2, 3 + 4], BF16)
        group = sb("group", [P, P], BF16)
        groupf = sb("groupf", [P, P])
        passed = sb("passed", [P, 3 + 4])
        npassed = sb("npassed", [P, 1])
        nextpat = sb("nextpat", [P, 4], I32)
        three = sb("three", [P, 4], I32)
        shifts = sb("shifts", [P, ROUNDS], I32)
        pattern = sb("pattern", [P, ROUNDS + 1, 4], I32)
        cand = sb("cand", [P, 2, 4], I32)
        thr8 = sb("thr8", [E, E])
        thrb = sb("thrb", [P, E])
        before = sb("before", [P, P], BF16)
        beforef = sb("beforef", [P, P])
        onesb = sb("onesb", [P, P], BF16)
        keep = sb("keep", [P, E, 2 * B])
        taken = sb("taken", [P, E, 2, B], BF16)
        totals = sb("totals", [P, 2 * E * B])
        slot = sb("slot", [P, E, 2, B])
        slot2 = sb("slot2", [P, E, 2, B])
        sloti = sb("sloti", [P, E, B], I32)
        slotlo = sb("slotlo", [P, E, B], I32)
        slothi = sb("slothi", [P, E, B], I32)
        iota = sb("iota", [P, P], I32)
        iotab = sb("iotab", [P, B], I32)
        iotap = sb("iotap", [P, 1], I32)
        pcol = sb("pcol", [P, 1])
        hot8 = sb("hot8", [P, B, SB], BF16)
        tokens = sb("tokens", [P, B, SB, 2], BF16)
        idx = sb("idx", [P, E, SB], I32)
        yb = VOT[:, 0, 0:SB * P].rearrange("p (s d) -> p s d", s=SB)
        stf = sb("stf", [P, B, 6])
        mvf = sb("mvf", [P, B, 2])
        vef = sb("vef", [P, B])
        rsf = sb("rsf", [P, B])
        nmf = sb("nmf", [P, B])

        self_in = sem("self_in")
        heads_in = [sem(f"heads_in{k}") for k in range(3)]
        wo_in = sem("wo_in")
        small_in = sem("small_in")
        route_in = sem("route_in")
        x_in = [sem(f"x_in{k}") for k in range(2)]
        c_in = [sem(f"c_in{k}") for k in range(2)]
        consts = sem("consts")
        setup_full = sem("setup_full")
        setup_dve = sem("setup_dve")
        setup_act = sem("setup_act")
        full = [sem(f"ring_full{k}") for k in range(RING_BANKS)]
        free = [sem(f"ring_free{k}") for k in range(RING_BANKS)]
        ct_hi = sem("ct_hi")
        self_full = sem("self_full")
        self_free = sem("self_free")
        s2_full = sem("s2_full")
        s2_free = sem("s2_free")
        cmax_done = sem("cmax_done")
        cexp_done = sem("cexp_done")
        csum_done = sem("csum_done")
        crcp_done = sem("crcp_done")
        pn_done = sem("pn_done")
        smax_done = sem("smax_done")
        snb_done = sem("snb_done")
        sexp_done = sem("sexp_done")
        srcp_done = sem("srcp_done")
        xbo_done = sem("xbo_done")
        ln1_steps = sem("ln1_steps")
        ln2_steps = sem("ln2_steps")
        r2_done = sem("r2_done")
        var1 = sem("var1")
        rstd1 = sem("rstd1")
        var2 = sem("var2")
        rstd2 = sem("rstd2")
        x1_done = sem("x1_done")
        x2_done = sem("x2_done")
        stored = [sem(f"stored{k}") for k in range(2)]
        passed_dve = sem("passed_dve")
        passed_sp = sem("passed_sp")
        chain = sem("chain")
        attended = sem("attended")
        w1_in = sem("w1_in")
        w2_in = sem("w2_in")
        g_sub = sem("g_sub")
        g_exp = sem("g_exp")
        gates_done = sem("gates_done")
        late_full = sem("late_full")
        late_done = sem("late_done")
        gates_stored = sem("gates_stored")
        gatesT_full = sem("gatesT_full")
        counted = sem("counted")
        summed = sem("summed")
        thr8_done = sem("thr8_done")
        thrb_full = sem("thrb_full")
        taken_done = sem("taken_done")
        prefix_full = sem("prefix_full")
        onehot_done = sem("onehot_done")
        tokens_done = sem("tokens_done")
        list_full = sem("list_full")
        idx_done = sem("idx_done")
        gathered = [[sem(f"gathered{b}_{h}") for h in range(SB)] for b in range(3)]
        xeT_full = sem("xeT_full")
        xeT_done = sem("xeT_done")
        hid_full = sem("hid_full")
        hid_done = sem("hid_done")
        ye_full = sem("ye_full")
        ye_added = sem("ye_added")
        ye_done = sem("ye_done")
        scattered = sem("scattered")
        fin_in = [sem(f"fin_in{c}") for c in range(B // 4)]
        fin_var = sem("fin_var")
        fin_rstd = sem("fin_rstd")
        fin_shifted = sem("fin_shifted")
        fin_done = sem("fin_done")
        fin_pool = sem("fin_pool")
        fin_dve = sem("fin_dve")
        out_done = sem("out_done")
        table = nc.dram_tensor("table", [TOKENS, ROW], F32, kind="Internal").ap()
        total = nc.dram_tensor("total", [TOKENS, P], F32, kind="Internal").ap()

        x_pairs = x.rearrange("(q e) t d -> q t e d", e=2)
        c_pairs = ctx_1024.rearrange("(q e) s d -> q s e d", e=2)

        def ring_wait_free(eng, at, name):
            wait(eng, free[bank_of(at, name)], fills_before(at, name))

        def ring_wait_full(eng, at, name):
            wait(eng, full[bank_of(at, name)], fills_before(at, name) + 1)

        def ring_wait_copied(eng, at, name):
            wait(eng, free[bank_of(at, name)], fills_before(at, name) + 1)

        HID_BANKS = (5, 6, 0)
        CONSTS = 19 + 2 * (P // E) - 1 + 3

        SETUP = ([("self", 0, 0), ("fold", 0, 0)] + [("turn", w, g) for w in range(2) for g in range(2)]
                 + [("M", 0, g) for g in range(4)] + [("turn", 2, g) for g in range(2)] + [("N", 2, g) for g in range(4)])

        def setup_wait_copied(eng, k):
            if k in DVE_UNITS:
                eng.wait_ge(setup_dve, DVE_UNITS.index(k) + 1)
            else:
                eng.wait_ge(setup_act, ACT_UNITS.index(k) + 1)

        def setup_copy(k, copy):
            kind, w, g = SETUP[k]
            src = PS[:, k % 8, :]
            if kind == "self":
                copy(wT[:, :, :].rearrange("p a b -> p (a b)"), src[:, 0:3 * P], 1.0)
            elif kind == "fold":
                copy(wvo[:, :, :].rearrange("p a b -> p (a b)"), src[:, 0:2 * P], 1.0)
            elif kind == "turn":
                copy(wheadsT[:, w, 4 * g:4 * g + 4, :].rearrange("p a b -> p (a b)"), src, 1.0)
            else:
                hi, lo = [t.rearrange("p (b i a) d -> p b a i d", a=2, i=4)[:, g // 2, g % 2, :, :]
                          for t in (MT if kind == "M" else NN)]
                copy((hi, lo), src.rearrange("p (i d) -> p i d", d=P), CROSS_SCALE if kind == "M" else 1.0)

        PRODUCTS = [k for k, (kind, _, _) in enumerate(SETUP) if kind in "MN"]
        ACT_UNITS = [k for k in range(len(SETUP)) if k in PRODUCTS or k % 2]
        DVE_UNITS = [k for k in range(len(SETUP)) if k in PRODUCTS or not k % 2]

        block = ctx.enter_context(nc.Block())

        @block.sync
        def _(sp):
            for k, w in enumerate((Wq, Wk, Wv, Wo)):
                sp.dma_start(wself[:, k, :], w).then_inc(self_in, 16)
            for k, w in enumerate((W_Q, W_K)):
                sp.dma_start(wheads[:, k, :].rearrange("m (h k) -> m h k", h=HEADS),
                             w.rearrange("h m k -> m h k")).then_inc(heads_in[k], 16)
            sp.dma_start(wheads[:, 2, :].rearrange("m (h k) -> m h k", h=HEADS),
                         W_V.rearrange("h m k -> m h k")).then_inc(heads_in[2], 16)
            for k in range(2):
                sp.dma_start(cin[k][:, :, :], c_pairs[k]).then_inc(c_in[k], 16)
            sp.dma_start(won[:, :, :], W_O.rearrange("(c p) o -> p c o", p=P)).then_inc(wo_in, 16)
            sp.dma_start(xin[0][:, :, :], x_pairs[0]).then_inc(x_in[0], 16)

            def load(at, q):
                if not (isinstance(q, int) and q < 2):
                    wait_apart(sp, full[bank_of(step_before(at), "xT")], fills_before(step_before(at), "xT") + 1, passed_sp)
                    wait_apart(sp, xbo_done, at[0] + 2, passed_sp)
                parity = at[1]
                sp.dma_start(xin[1 - parity][:, :, :], x_pairs[q]).then_inc(x_in[1 - parity], 16)

            def load_context(at, q):
                at = step_before(at)
                wait_apart(sp, full[bank_of(at, "cT")], fills_before(at, "cT") + 1, passed_sp)
                for k in range(2):
                    sp.dma_start(cin[k][:, :, :], c_pairs[q + k]).then_inc(c_in[k], 16)

            def store(q, parity):
                wait_apart(sp, x2_done, 2 * q + 2, passed_sp)
                rows = 2 * P
                tab = table.rearrange("(q e t) d -> q t e d", e=2, t=P)
                sm = total.rearrange("(q e t) d -> q t e d", e=2, t=P)
                sp.dma_start(tab[q, :, :, 0:P], x2[parity][:, :, :]).then_inc(stored[parity], 16)
                sp.dma_start(sm[q], x2[parity][:, :, :]).then_inc(stored[parity], 16)

            def step(p, parity, nth, ahead, prep, cross, post):
                if not isinstance(p, int) or p + 3 < PAIRS:
                    load((p, parity, nth), p + 3)
                if parity == 1 and (not isinstance(p, int) or p + 3 < PAIRS):
                    load_context((p, parity, nth), p + 3)
                if post:
                    store(p - 1, 1 - parity)

            attention_steps(sp, step)
            sp.dma_start(w1[:, :, :], W1.rearrange("e d f -> d e f")).then_inc(w1_in, 16)
            sp.dma_start(w2[:, :, :, :].rearrange("p e c d -> p (e c) d"),
                         W2.rearrange("e (c p) d -> p (e c) d", p=P)).then_inc(w2_in, 16)
            for k in range(2):
                sp.wait_ge(stored[k], 32 * PAIRS // 2)
            sp.wait_ge(gates_done, 1)
            sp.dma_start(table.rearrange("(b t) d -> t b d", t=P)[:, :, P:ROW], gates[:, :, :]).then_inc(gates_stored, 16)
            sp.wait_ge(scattered, 16 * SB * E)
            rows = total.rearrange("(b t) d -> t b d", t=P)
            for c in range(B // 4):
                sp.dma_start(fin[:, 4 * c:4 * c + 4, :], rows[:, 4 * c:4 * c + 4, :]).then_inc(fin_in[c], 16)
            for c in range(B // 4):
                sp.wait_ge(fin_done, sum(by_act(k) for k in range(c + 1)))
                sp.wait_ge(fin_pool, c // 2 + 1)
                if c == B // 4 - 1:
                    sp.wait_ge(fin_dve, 1)
                sp.dma_start(out.rearrange("b t d -> t b d")[:, 4 * c:4 * c + 4, :],
                             fin[:, 4 * c:4 * c + 4, :]).then_inc(out_done, 16)
            sp.wait_ge(gates_stored, 16)
            sp.wait_ge(out_done, 16 * (B // 4))

        def blocks_through(e, n):
            return 2 * e + 1 + (n if e == E - 1 else n // 4)

        def y_bank(e, h, s):
            if e == E - 1:
                return PS[:, (1, 2, 3, 4)[s], h * P:(h + 1) * P]
            return PS[:, 1 + h, s * P:(s + 1) * P]

        @block.gpsimd
        def _(pool):
            pool.memset(ident[:, :], 0.0).then_inc(consts, 1)
            pool.memset(ones[:, :], 1.0).then_inc(consts, 1)
            pool.wait_ge(consts, 1)
            pool.affine_select(out=ident[:, :], in_=ident[:, :], compare_op=ALU.not_equal, fill=1.0,
                               base=0, pattern=[[-1, P]], channel_multiplier=1).then_inc(consts, 1)
            pool.memset(mhalf[:, :], -0.5).then_inc(consts, 1)
            pool.memset(VOT[:, :, HK:HKP], 0.0).then_inc(consts, 1)
            pool.memset(pn[:, :, HK:HKP], 0.0).then_inc(consts, 1)
            pool.iota(iota[:, :], [[1, P]], base=0, channel_multiplier=0).then_inc(consts, 1)
            pool.iota(iotab[:, :], [[P, B]], base=0, channel_multiplier=0).then_inc(consts, 1)
            pool.iota(iotap[:, :], [[1, 1]], base=0, channel_multiplier=1).then_inc(consts, 1)
            pool.memset(three[:, 3:4], 0).then_inc(consts, 1)
            pool.iota(three[:, 0:3], [[1, 3]], base=1, channel_multiplier=0).then_inc(consts, 1)
            pool.iota(shifts[:, 0:LEFTS], [[-2, LEFTS]], base=answer_shift(0), channel_multiplier=0).then_inc(consts, 1)
            pool.iota(shifts[:, LEFTS:ROUNDS], [[2, ROUNDS - LEFTS]], base=-answer_shift(LEFTS),
                      channel_multiplier=0).then_inc(consts, 1)
            pool.memset(count[:, :, 3:7], float(TOPK)).then_inc(consts, 1)
            pool.memset(groupf[:, :], 0.0).then_inc(consts, 1)
            pool.memset(beforef[:, :], 0.0).then_inc(consts, 1)
            pool.memset(keep[:, :, :], 1.0).then_inc(consts, 1)
            pool.memset(onesb[:, :], 1.0).then_inc(consts, 1)
            pool.wait_ge(consts, 18)
            pool.memset(keep[:, :, 0:1], 0.0).then_inc(consts, 1)
            v = groupf[:, :].rearrange("p (a e) -> p a e", e=E)
            for n in range(-(P // E) + 1, P // E):
                pool.affine_select(out=v, in_=v, compare_op=ALU.not_equal, fill=1.0, base=E * n,
                                   pattern=[[-E, P // E], [-1, E]], channel_multiplier=1).then_inc(consts, 1)
                pool.wait_ge(consts, 19 + n + P // E)
            pool.affine_select(out=beforef[:, :], in_=beforef[:, :], compare_op=ALU.is_gt, fill=-1.0, base=0,
                               pattern=[[1, P]], channel_multiplier=-1).then_inc(consts, 1)
            pool.tensor_copy(pcol[:, :], iotap[:, :]).then_inc(consts, 1)
            pool.wait_ge(consts, CONSTS - 1)
            pool.tensor_copy(before[:, :], beforef[:, :]).then_inc(consts, 1)
            pool.wait_ge(setup_act, 1)

            def step(p, parity, nth, ahead, prep, cross, post):
                if prep:
                    wait(pool, x_in[1 - parity], 16 * (nth + 1))
                    for e in range(2):
                        i = pool.tensor_tensor(xbo[:, e, :], xin[1 - parity][:, e, :], wvo[:, 1, :], ALU.add)
                    i.then_inc(xbo_done, 1)
                if cross:
                    for e in range(2):
                        wait(pool, crcp_done, 2 * p + e + 1)
                        pool.tensor_tensor(
                            pn[:, e, 0:HK].rearrange("p (h k) -> p h k", h=HEADS),
                            pc[:, e, :].rearrange("p (h k) -> p h k", h=HEADS),
                            crcp[:, e, :].unsqueeze(2).to_broadcast([P, HEADS, KEYS]),
                            ALU.mult).then_inc(pn_done, 1)
                if prep:
                    wait(pool, var1, p + 2)
                    pool.tensor_tensor(rs1[:, :], ve1[:, :], mhalf[:, :], ALU.pow).then_inc(rstd1, 1)
                if cross:
                    for e in range(2):
                        wait(pool, var2, 2 * p + e + 1)
                        pool.tensor_tensor(rs2[:, e:e + 1], ve2[:, e:e + 1], mhalf[:, 0:1], ALU.pow).then_inc(rstd2, 1)

            attention_steps(pool, step)

            def gather(e, first=0, end=SB):
                pool.wait_ge(idx_done, e + 1)
                if e == 0:
                    pool.wait_ge(gates_stored, 16)
                    for k in range(2):
                        pool.wait_ge(stored[k], 32 * PAIRS // 2)
                if e >= 3:
                    pool.wait_ge(ye_done, 2 * (e - 2))
                for h in range(first, end):
                    pool.indirect_dma_start(xg[:, e % 3, h, :], None, table,
                                            bass.IndirectOffsetOnAxis(ap=idx[:, e, h:h + 1], axis=0)
                                            ).then_inc(gathered[e % 3][h], 16)

            def scatter(e):
                if e:
                    pool.wait_ge(scattered, 16 * SB * e)
                for h in range(SB):
                    pool.wait_ge(ye_done, blocks_through(e, h))
                    pool.indirect_dma_start(total, bass.IndirectOffsetOnAxis(ap=idx[:, e, h:h + 1], axis=0),
                                            ye[:, e % 2, h, :], None, compute_op=ALU.add).then_inc(scattered, 16)

            gather(0)
            gather(1)
            for e in range(E):
                if e + 2 < E - 1:
                    gather(e + 2)
                elif e + 2 == E - 1:
                    gather(E - 1, 0, SB - 2)
                scatter(e)
                if e + 2 == E - 1:
                    gather(E - 1, SB - 2, SB)

            def fin_last_batch(c):
                pool.wait_ge(fin_rstd, c + 1)
                b = 4 * c + 3
                pool.tensor_scalar(fin[:, b, :], fin[:, b, :], mvf[:, b, 0:1], rsf[:, b:b + 1],
                                   ALU.subtract, ALU.mult).then_inc(fin_pool, 1)

            for c in range(B // 4):
                pool.wait_ge(fin_var, c + 1)
                pool.tensor_tensor(rsf[:, 4 * c:4 * c + 4], vef[:, 4 * c:4 * c + 4],
                                   mhalf[:, 0:1].to_broadcast([P, 4]), ALU.pow).then_inc(fin_rstd, 1)
                if c % 2 == 0:
                    fin_last_batch(c)

        @block.scalar
        def _(act):
            act.dma_start(brow[:, 0:P], bo.rearrange("(a n) -> a n", a=1)).then_inc(small_in, 16)
            for k, b in enumerate((bq, bk, bv)):
                act.dma_start(bcol[:, k:k + 1], b.rearrange("(n a) -> n a", a=1)).then_inc(small_in, 16)
            act.dma_start(wr[:, :], Wr).then_inc(route_in, 16)
            act.dma_start(b1n[:, :], b1.rearrange("e (c f) -> (e c) f", f=P)).then_inc(route_in, 16)
            act.dma_start(brow[:, P:P + E * P], b2.rearrange("(a e) d -> a (e d)", a=1)).then_inc(route_in, 16)
            def set_up(dst, src, scale):
                if isinstance(dst, tuple):
                    dst = dst[0]
                act.activation(dst, src, ACT.Copy, scale=scale).then_inc(setup_act, 1)

            for k in ACT_UNITS:
                act.wait_ge(setup_full, k + 1)
                setup_copy(k, set_up)

            def copy(at, name, dst, src):
                ring_wait_full(act, at, name)
                act.activation(dst, src, ACT.Copy).then_inc(free[bank_of(at, name)], 1)

            def step(p, parity, nth, ahead, prep, cross, post):
                at = (p, parity, nth)

                def bank(name):
                    return ring[bank_of(at, name)]

                def heads_copy(first, last):
                    for h in range(first, last):
                        if h in BY_DVE:
                            continue
                        name = ("A" if parity else "VOT", h)
                        copy(at, name, (A if parity else VOT)[:, :, h * KEYS:(h + 1) * KEYS],
                             bank(name)[:, 0:4 * KEYS].rearrange("p (b k) -> p b k", b=4))

                def cross_exp(e):
                    wait(act, s2_free, 2 * p + e + 1)
                    act.activation(pc[:, e, :], pc[:, e, :], ACT.Exp).then_inc(cexp_done, 1)

                def cross_pT(e):
                    for g, (a, b) in enumerate(GROUPS):
                        name = ("P2T", e, g)
                        copy(at, name, pT[:, e, a * P:b * P], bank(name)[:, 0:(b - a) * P])

                def logits_copy():
                    copy(at, "LG", logits[:, bass.ds(2 * (p - 1), 2), :].rearrange("p e n -> p (e n)"),
                         bank("LG")[:, 0:2 * E])

                def vo_copy(pair, e):
                    for g, (a, b) in enumerate(GROUPS):
                        name = ("VO", pair, e, g)
                        copy(at, name, VO[pair][:, e, a:b, :].rearrange("p c d -> p (c d)"), bank(name)[:, 0:(b - a) * P])

                def self_exp():
                    wait(act, snb_done, p + 2)
                    for e in range(2):
                        act.activation(pself[:, e, :], small[:, e * P:(e + 1) * P], ACT.Exp, bias=snb[:, e:e + 1],
                                       scale=SELF_SCALE, accum_out=ssum[:, e:e + 1]).then_inc(sexp_done, 1)

                def self_pT():
                    wait(act, self_full, 4 * (p + 1) + 2)
                    act.activation(pselfT[:, :, :].rearrange("p e t -> p (e t)"), small[:, 0:2 * P],
                                   ACT.Copy).then_inc(self_free, 1)

                first = prep and not cross
                even, odd = ahead and parity == 0, prep and parity == 1
                heads = even or odd
                if parity == 0 and prep:
                    vo_copy(1, 1)
                if even:
                    ring_wait_full(act, at, "cT")
                    act.activation(cT[0][:, :], bank("cT")[:, 0:4 * KEYS], ACT.Copy).then_inc(ct_hi, 1)
                if prep:
                    ring_wait_full(act, at, "QK")
                    act.activation(qT[:, :, :].rearrange("p e t -> p (e t)"), bank("QK")[:, 0:2 * P], ACT.Identity,
                                   bias=bcol[:, 0:1])
                    act.activation(kT[:, :, :].rearrange("p e t -> p (e t)"), bank("QK")[:, 2 * P:4 * P], ACT.Identity,
                                   bias=bcol[:, 1:2]).then_inc(free[bank_of(at, "QK")], 1)
                    copy(at, "V", vs[:, :, :].rearrange("p e t -> p (e t)"), bank("V")[:, 0:2 * P])
                if post:
                    copy(at, "x2T", x2T[:, :, :].rearrange("p e t -> p (e t)"), bank("x2T")[:, 0:2 * P])
                if odd:
                    vo_copy(0, 0)
                    if first:
                        self_exp()
                    vo_copy(0, 1)
                    if first:
                        self_pT()
                if cross:
                    cross_exp(0)
                if heads:
                    heads_copy(0, 4)
                if post and parity == 1:
                    logits_copy()
                if heads:
                    heads_copy(4, 7)
                if prep and cross:
                    self_exp()
                if heads:
                    heads_copy(7, 8)
                if cross:
                    cross_exp(1)
                if prep and cross:
                    self_pT()
                if heads:
                    heads_copy(8, 12)
                if cross:
                    cross_pT(0)
                if heads:
                    heads_copy(12, 16)
                if ahead and parity == 1:
                    copy(at, "xT", xT[:, :, :].rearrange("p e t -> p (e t)"), bank("xT")[:, 0:2 * P])
                if cross:
                    cross_pT(1)
                if post and parity == 0:
                    logits_copy()
                if even:
                    copy(at, "xT", xT[:, :, :].rearrange("p e t -> p (e t)"), bank("xT")[:, 0:2 * P])
                if odd:
                    vo_copy(1, 0)
                if prep:
                    wait(act, self_full, 4 * (p + 1) + 4)
                    act.activation(x1T[:, :, :].rearrange("p e t -> p (e t)"), small[:, 0:2 * P],
                                   ACT.Copy).then_inc(self_free, 1)

            act.wait_ge(small_in, 16 * 4)
            attention_steps(act, step)

            act.wait_ge(g_sub, 1)
            act.activation(gates[:, :, :], gates[:, :, :], ACT.Exp).then_inc(g_exp, 1)
            act.wait_ge(late_full, 1)
            act.activation(b1T[:, :], PS[:, 4, 0:E * FC], ACT.Copy).then_inc(late_done, 1)
            act.activation(group[:, :], PS[:, 4, P:2 * P], ACT.Copy).then_inc(late_done, 1)
            act.wait_ge(late_full, 3)
            act.activation(b2b[:, :, :].rearrange("p (a b) d -> p a (b d)", a=2), PS[:, 5:7, :],
                           ACT.Copy).then_inc(late_done, 1)

            def copy_rows(e, h):
                act.wait_ge(xeT_full, 2 * e + h + 1)
                act.activation(xeT[:, 512 * h:512 * h + 512], PS[:, 3 + h, :], ACT.Copy).then_inc(xeT_done, 1)

            for e in range(E):
                copy_rows(e, 0)
                if 0 < e < E - 1:
                    copy_rows(e, 1)
                for n in range(2 * FC):
                    h, c = divmod(n, FC)
                    if e in (0, E - 1) and n == FC:
                        copy_rows(e, 1)
                    act.wait_ge(hid_full, 2 * FC * e + n + 1)
                    act.activation(hid[:, c, 512 * h:512 * h + 512], PS[:, HID_BANKS[(2 * FC * e + n) % 3], :], ACT.Gelu,
                                   bias=b1T[:, FC * e + c:FC * e + c + 1]).then_inc(hid_done, 1)

            for c in range(B // 4):
                act.wait_ge(fin_shifted, c + 1)
                for b in range(4 * c, 4 * c + by_act(c)):
                    act.activation(fin[:, b, :], fin[:, b, :], ACT.Identity, bias=nmf[:, b:b + 1],
                                   scale=rsf[:, b:b + 1]).then_inc(fin_done, 1)

        @block.vector
        def _(dve):
            dve.wait_ge(consts, 11)
            for r in range(ROUNDS + 1):
                shift = max(2 * (ROUNDS - 1 - r), 0)
                if r == 0:
                    i = dve.tensor_scalar(pattern[:, r, :], three[:, :], shift, None, ALU.logical_shift_left)
                elif r < ROUNDS:
                    i = dve.tensor_scalar(pattern[:, r, :], three[:, :], shift, shifted_four(r - 1),
                                          ALU.logical_shift_left, ALU.bitwise_xor)
                else:
                    i = dve.tensor_scalar(pattern[:, r, :], three[:, :], 0, shifted_four(r - 1),
                                          ALU.bitwise_and, ALU.bitwise_xor)
            i.then_inc(chain, 1)

            def set_up(dst, src, scale):
                if isinstance(dst, tuple):
                    dve.scalar_tensor_tensor(out=dst[1], in0=src, scalar=scale, in1=dst[0].bitcast(F32),
                                             op0=ALU.mult, op1=ALU.subtract).then_inc(setup_dve, 1)
                else:
                    dve.tensor_copy(dst, src).then_inc(setup_dve, 1)

            for k in DVE_UNITS:
                dve.wait_ge(setup_full, k + 1)
                if k in PRODUCTS:
                    dve.wait_ge(setup_act, ACT_UNITS.index(k) + 1)
                setup_copy(k, set_up)

            def step(p, parity, nth, ahead, prep, cross, post):
                def second_norm(q, e, par, earlier):
                    wait(dve, rstd2, 2 * q + e + 1)
                    wait(dve, stored[par], 32 * earlier)
                    dve.tensor_scalar(x2[par][:, e, :], r2[:, e, :], mv2[:, e, 0:1], rs2[:, e:e + 1],
                                      ALU.subtract, ALU.mult).then_inc(x2_done, 1)

                def cross_max(e):
                    wait(dve, s2_full, 2 * p + e + 1)
                    s = PS[:, 0:3, :].rearrange("p a b -> p (a b)")[:, 0:HK].rearrange("p (h k) -> p h k", h=HEADS)
                    dve.tensor_reduce(cmax[:, e, :], s, AX.X, ALU.max).then_inc(cmax_done, 1)

                def cross_sub(e):
                    wait(dve, cmax_done, 2 * p + e + 1)
                    s = PS[:, 0:3, :].rearrange("p a b -> p (a b)")[:, 0:HK].rearrange("p (h k) -> p h k", h=HEADS)
                    dve.tensor_tensor(pc[:, e, :].rearrange("p (h k) -> p h k", h=HEADS), s,
                                      cmax[:, e, :].unsqueeze(2).to_broadcast([P, HEADS, KEYS]),
                                      ALU.subtract).then_inc(s2_free, 1)

                def cross_sum(e):
                    wait(dve, cexp_done, 2 * p + e + 1)
                    dve.tensor_reduce(csum[:, e, :], pc[:, e, :].rearrange("p (h k) -> p h k", h=HEADS), AX.X,
                                      ALU.add).then_inc(csum_done, 1)
                    wait(dve, csum_done, 2 * p + e + 1)
                    dve.reciprocal(crcp[:, e, :], csum[:, e, :]).then_inc(crcp_done, 1)

                at = (p, parity, nth)

                def second_stats(e):
                    name = ("AV2", e)
                    ring_wait_full(dve, at, name)
                    dve.tensor_tensor(r2[:, e, :], ring[bank_of(at, name)][:, 0:P], x1[parity][:, e, :],
                                      ALU.add).then_inc(free[bank_of(at, name)], 1)
                    ring_wait_copied(dve, at, name)
                    dve.bn_stats(st2[:, e, :], r2[:, e, :]).then_inc(ln2_steps, 1)
                    wait_apart(dve, ln2_steps, 4 * p + 2 * e + 1, passed_dve)
                    dve.bn_aggr(mv2[:, e, :], st2[:, e, :]).then_inc(ln2_steps, 1)
                    wait(dve, ln2_steps, 4 * p + 2 * e + 2)
                    dve.tensor_scalar(ve2[:, e:e + 1], mv2[:, e, 1:2], EPS, None, ALU.add).then_inc(var2, 1)

                def first_norm():
                    wait(dve, sexp_done, 2 * (p + 1) + 2)
                    dve.reciprocal(srcp[:, :], ssum[:, :]).then_inc(srcp_done, 1)
                    wait(dve, srcp_done, p + 2)
                    wait(dve, xbo_done, p + 2)
                    wait(dve, self_full, 4 * (p + 1) + 3)
                    for e in range(2):
                        i = dve.scalar_tensor_tensor(out=r1[:, e, :], in0=small[:, e * P:(e + 1) * P],
                                                     scalar=srcp[:, e:e + 1], in1=xbo[:, e, :],
                                                     op0=ALU.mult, op1=ALU.add)
                    i.then_inc(self_free, 1)
                    wait(dve, self_free, 3 * (p + 1) + 2)
                    for e in range(2):
                        i = dve.bn_stats(st1[:, e, :], r1[:, e, :])
                    i.then_inc(ln1_steps, 1)
                    wait_apart(dve, ln1_steps, 2 * (p + 1) + 1, passed_dve)
                    for e in range(2):
                        i = dve.bn_aggr(mv1[:, e, :], st1[:, e, :])
                    i.then_inc(ln1_steps, 1)
                    wait(dve, ln1_steps, 2 * (p + 1) + 2)
                    dve.tensor_scalar(ve1[:, :], mv1[:, :, 1:2].rearrange("p e a -> p (e a)"), EPS, None,
                                      ALU.add).then_inc(var1, 1)

                def heads_copy(first, last):
                    for h in range(first, last):
                        if h not in BY_DVE:
                            continue
                        name = ("A" if parity else "VOT", h)
                        ring_wait_full(dve, at, name)
                        dve.tensor_copy((A if parity else VOT)[:, :, h * KEYS:(h + 1) * KEYS],
                                        ring[bank_of(at, name)][:, 0:4 * KEYS].rearrange("p (b k) -> p b k", b=4)
                                        ).then_inc(free[bank_of(at, name)], 1)

                even, odd = ahead and parity == 0, prep and parity == 1
                heads = even or odd
                if post:
                    second_norm(p - 1, 1, 1 - parity, nth - 1)
                if cross:
                    cross_max(0)
                    cross_sub(0)
                if even:
                    wait(dve, ct_hi, nth + 2)
                    dve.tensor_tensor(cT[1][:, :], ring[bank_of(at, "cT")][:, 0:4 * KEYS], cT[0][:, :].bitcast(F32),
                                      ALU.subtract).then_inc(free[bank_of(at, "cT")], 1)
                if cross:
                    cross_sum(0)
                if heads:
                    heads_copy(0, 4)
                if cross:
                    cross_max(1)
                if prep:
                    wait(dve, self_full, 4 * (p + 1) + 1)
                    dve.tensor_reduce(smax[:, :], small[:, 0:2 * P].rearrange("p (e k) -> p e k", e=2), AX.X,
                                      ALU.max).then_inc(smax_done, 1)
                    wait(dve, smax_done, p + 2)
                    dve.tensor_scalar(snb[:, :], smax[:, :], -SELF_SCALE, None, ALU.mult).then_inc(snb_done, 1)
                if cross:
                    cross_sub(1)
                if heads:
                    heads_copy(4, 12)
                if cross:
                    cross_sum(1)
                if heads:
                    heads_copy(12, 16)
                if prep:
                    first_norm()
                    wait(dve, rstd1, p + 2)
                    for e in range(2):
                        dve.tensor_scalar(x1[1 - parity][:, e, :], r1[:, e, :], mv1[:, e, 0:1], rs1[:, e:e + 1],
                                          ALU.subtract, ALU.mult).then_inc(x1_done, 1)
                if cross:
                    second_stats(0)
                    second_norm(p, 0, parity, nth - parity)
                    second_stats(1)

            attention_steps(dve, step)
            links = [1]

            def link(i):
                links[0] += 1
                i.then_inc(chain, 1)
                dve.wait_ge(chain, links[0])

            ring_wait_copied(dve, (PAIRS, 0, PAIRS // 2), "LG")
            link(dve.tensor_reduce(gmax[:, :], logits[:, :, :], AX.X, ALU.max))
            dve.tensor_tensor(gates[:, :, :], logits[:, :, :], gmax[:, :].unsqueeze(2).to_broadcast([P, B, E]),
                              ALU.subtract).then_inc(g_sub, 1)
            dve.wait_ge(g_exp, 1)
            link(dve.tensor_reduce(gsum[:, :], gates[:, :, :], AX.X, ALU.add))
            link(dve.reciprocal(grcp[:, :], gsum[:, :]))
            dve.tensor_tensor(gates[:, :, :], gates[:, :, :], grcp[:, :].unsqueeze(2).to_broadcast([P, B, E]),
                              ALU.mult).then_inc(gates_done, 1)
            dve.wait_ge(gatesT_full, 1)
            link(dve.tensor_copy(gatesT[:, :], PS[:, 0, 0:2 * P]))

            for r in range(ROUNDS):
                now = pattern[:, 0, :] if r == 0 else cand[:, r % 2, :]
                for j in range(3):
                    i = dve.tensor_scalar(above[:, j, :], gatesT[:, :], now[:, j:j + 1].bitcast(F32), None,
                                          ALU.is_ge, ALU.add, accum_out=count[:, r % 2, j:j + 1])
                i.then_inc(counted, 1)
                dve.tensor_tensor(nextpat[:, :], pattern[:, r + 1, :], now[:, 3:4].to_broadcast([P, 4]),
                                  ALU.bitwise_xor)
                dve.wait_ge(summed, r + 1)
                link(dve.tensor_scalar(passed[:, :], PS[:, 1, 0:7], float(TOPK), None, ALU.is_ge, ALU.add,
                                       accum_out=npassed[:, :]))
                link(dve.scalar_tensor_tensor(
                    out=cand[:, (r + 1) % 2, :], in0=npassed[:, :].bitcast(I32).to_broadcast([P, 4]),
                    scalar=shifts[:, r:r + 1], in1=nextpat[:, :],
                    op0=ALU.logical_shift_left if r < LEFTS else ALU.logical_shift_right, op1=ALU.bitwise_xor))
            dve.tensor_scalar(thr8[:, :], ident[0:E, 0:E], cand[0:E, ROUNDS % 2, 3:4].bitcast(F32), None,
                              ALU.mult).then_inc(thr8_done, 1)
            dve.wait_ge(thrb_full, 1)
            link(dve.tensor_copy(thrb[:, :], PS[:, 1, 8:8 + E]))
            g = gates[:, :, :].rearrange("p b e -> p e b")
            t = thrb[:, :].unsqueeze(2).to_broadcast([P, E, B])
            dve.tensor_tensor(taken[:, :, 0, :], g, t, ALU.is_gt)
            dve.tensor_tensor(taken[:, :, 1, :], g, t, ALU.is_equal).then_inc(taken_done, 1)
            dve.wait_ge(prefix_full, 1)
            def slots(a, z):
                flat = "p e a b -> p (e a b)"
                part = slice(2 * B * a, 2 * B * z)
                link(dve.tensor_tensor_scan(totals[:, part], keep[:, :, :].rearrange("p n b -> p (n b)")[:, part],
                                            PS[:, 3, part], 0.0, ALU.mult, ALU.add))
                link(dve.tensor_tensor(slot2[:, a:z, :, :].rearrange(flat), PS[:, 2, part], totals[:, part], ALU.add))
                link(dve.scalar_tensor_tensor(out=slot[:, a:z, :, :].rearrange(flat),
                                              in0=slot2[:, a:z, :, :].rearrange(flat), scalar=-NONE,
                                              in1=taken[:, a:z, :, :].rearrange(flat), op0=ALU.add, op1=ALU.mult))
                link(dve.scalar_tensor_tensor(out=sloti[:, a:z, :], in0=slot[:, a:z, 0, :], scalar=NONE,
                                              in1=slot[:, a:z, 1, :], op0=ALU.add, op1=ALU.add))
                dve.tensor_scalar(slotlo[:, a:z, :], sloti[:, a:z, :], P - 1, None, ALU.bitwise_and)
                link(dve.tensor_scalar(slothi[:, a:z, :], sloti[:, a:z, :], 7, None, ALU.logical_shift_right))

            def one_hots(e):
                if e:
                    dve.wait_ge(list_full, e)
                link(dve.tensor_tensor(hot8[:, :, :], slothi[:, e, :].unsqueeze(2).to_broadcast([P, B, SB]),
                                       iota[:, 0:SB].unsqueeze(1).to_broadcast([P, B, SB]), ALU.is_equal))
                dve.tensor_tensor(tokens[:, :, :, 0], hot8[:, :, :],
                                  iotab[:, :].unsqueeze(2).to_broadcast([P, B, SB]), ALU.mult)
                dve.tensor_scalar(tokens[:, :, :, 1], hot8[:, :, :], pcol[:, 0:1], None, ALU.mult).then_inc(tokens_done, 1)
                for q in range(4):
                    b = B // 4 * q
                    dve.tensor_tensor(onehot[:, b:b + B // 4, :], iota[:, :].unsqueeze(1).to_broadcast([P, B // 4, P]),
                                      slotlo[:, e, b:b + B // 4].unsqueeze(2).to_broadcast([P, B // 4, P]),
                                      ALU.is_equal).then_inc(onehot_done, 1)

            def make_idx(e):
                dve.wait_ge(list_full, e + 1)
                with nc.allow_low_precision(reason="numbers of tokens are whole and below 2 ** 24"):
                    dve.tensor_reduce(idx[:, e, :], PS[:, 7, 0:2 * SB].rearrange("p (s a) -> p s a", a=2), AX.X,
                                      ALU.add).then_inc(idx_done, 1)

            def last_results():
                e = E - 1
                dve.wait_ge(scattered, 16 * SB * (e - 1))
                for n in range(SB):
                    dve.wait_ge(ye_full, blocks_through(e, n))
                    dve.tensor_tensor(yb[:, n, :], y_bank(e, n // 4, n % 4), b2b[:, e, :], ALU.add).then_inc(ye_added, 1)
                    dve.wait_ge(ye_added, blocks_through(e, n))
                    dve.wait_ge(gathered[e % 3][n], 16 * (e // 3 + 1))
                    dve.tensor_scalar(ye[:, e % 2, n, :], yb[:, n, :], xg[:, e % 3, n, P + e:P + e + 1], None,
                                      ALU.mult).then_inc(ye_done, 1)

            def results(e, h):
                if e >= 2:
                    dve.wait_ge(scattered, 16 * SB * (e - 1))
                dve.wait_ge(ye_full, 2 * e + h + 1)
                dve.tensor_tensor(yb[:, 4 * h:4 * h + 4, :], PS[:, 1 + h, :].rearrange("p (s d) -> p s d", d=P),
                                  b2b[:, e:e + 1, :].to_broadcast([P, 4, P]), ALU.add).then_inc(ye_added, 1)
                dve.wait_ge(ye_added, 2 * e + h + 1)
                for s in range(4 * h, 4 * h + 4):
                    dve.wait_ge(gathered[e % 3][s], 16 * (e // 3 + 1))
                dve.tensor_tensor(ye[:, e % 2, 4 * h:4 * h + 4, :], yb[:, 4 * h:4 * h + 4, :],
                                  xg[:, e % 3, 4 * h:4 * h + 4, P + e:P + e + 1].to_broadcast([P, 4, P]),
                                  ALU.mult).then_inc(ye_done, 1)

            slots(0, 1)
            one_hots(0)
            slots(1, E)
            make_idx(0)
            for e in range(1, 3):
                one_hots(e)
                make_idx(e)
            for e in range(E - 1):
                if e + 3 < E:
                    one_hots(e + 3)
                results(e, 0)
                if e + 3 < E:
                    make_idx(e + 3)
                results(e, 1)
            last_results()

            def fin_shift(c):
                dve.wait_ge(fin_rstd, c + 1)
                dve.scalar_tensor_tensor(out=nmf[:, 4 * c:4 * c + 4],
                                         in0=mvf[:, 4 * c:4 * c + 4, 0:1].rearrange("p b a -> p (b a)"), scalar=-1.0,
                                         in1=rsf[:, 4 * c:4 * c + 4], op0=ALU.mult, op1=ALU.mult).then_inc(fin_shifted, 1)

            for c in range(B // 4):
                dve.wait_ge(fin_in[c], 16)
                for b in range(4 * c, 4 * c + 4):
                    i = dve.bn_stats(stf[:, b, :], fin[:, b, :])
                link(i)
                for b in range(4 * c, 4 * c + 4):
                    i = dve.bn_aggr(mvf[:, b, :], stf[:, b, :])
                link(i)
                dve.tensor_scalar(vef[:, 4 * c:4 * c + 4], mvf[:, 4 * c:4 * c + 4, 1:2].rearrange("p b a -> p (b a)"), EPS,
                                  None, ALU.add).then_inc(fin_var, 1)
                if c:
                    fin_shift(c - 1)
            fin_shift(B // 4 - 1)
            for b in (B - 2, B - 1):
                i = dve.tensor_scalar(fin[:, b, :], fin[:, b, :], mvf[:, b, 0:1], rsf[:, b:b + 1],
                                      ALU.subtract, ALU.mult)
            i.then_inc(fin_dve, 1)

        @block.tensor
        def _(pe):
            pe.wait_ge(consts, 2)

            def keep_warm(n, bank=7):
                for _ in range(n):
                    pe.matmul(PS[:, bank, 0:P], ones[:, :], ones[:, :], start=True, stop=True)

            keep_warm(WARM["start"])
            pe.wait_ge(consts, 4)
            for k, (kind, w, g) in enumerate(SETUP):
                if k >= 8:
                    setup_wait_copied(pe, k - 8)
                bank = PS[:, k % 8, :]
                if kind == "self":
                    pe.wait_ge(self_in, 16 * 4)
                    for j, n in enumerate((0, 1, 3)):
                        i = pe.transpose(bank[:, j * P:(j + 1) * P], wself[:, n, :], ident[:, :])
                elif kind == "fold":
                    pe.wait_ge(small_in, 16 * 4)
                    setup_wait_copied(pe, 0)
                    pe.matmul(bank[:, 0:P], wself[:, 2, :], wT[:, 2, :], start=True, stop=True)
                    pe.matmul(bank[:, P:2 * P], bcol[:, 2:3].to_broadcast([P, P]), wT[:, 2, :], start=True, stop=False)
                    i = pe.matmul(bank[:, P:2 * P], ones[0:1, :], brow[0:1, 0:P], start=False, stop=True)
                elif kind == "turn":
                    if g == 0:
                        pe.wait_ge(heads_in[w], 16)
                    for j in range(4):
                        c = 4 * g + j
                        i = pe.transpose(bank[:, j * P:(j + 1) * P], wheads[:, w, c * P:(c + 1) * P], ident[:, :])
                else:
                    for w in ((0, 1) if kind == "M" else (2,)):
                        setup_wait_copied(pe, SETUP.index(("turn", w, g // 2)))
                    if kind == "N" and g == 0:
                        pe.wait_ge(wo_in, 16)
                    lo = DK * (g % 2)
                    for j in range(4):
                        c = 4 * (g // 2) + j
                        lhsT = wheadsT[lo:lo + DK, 1 if kind == "M" else 2, c, :]
                        rhs = wheadsT[lo:lo + DK, 0, c, :] if kind == "M" else won[lo:lo + DK, c, :]
                        i = pe.matmul(bank[:, j * P:(j + 1) * P], lhsT, rhs, start=True, stop=True)
                i.then_inc(setup_full, 1)
                keep_warm(WARM.get(SETUP[k], 0))
            setup_wait_copied(pe, 8)
            keep_warm(WARM["end"], 0)
            setup_wait_copied(pe, len(SETUP) - 2)
            setup_wait_copied(pe, len(SETUP) - 1)
            pe.wait_ge(consts, 6)
            pe.wait_ge(route_in, 16 * 3)

            def step(p, parity, nth, ahead, prep, cross, post):
                at = (p, parity, nth)

                def unit(name):
                    ring_wait_free(pe, at, name)
                    return ring[bank_of(at, name)]

                def done(i, name):
                    i.then_inc(full[bank_of(at, name)], 1)

                def heads(first, last):
                    for h in range(first, last):
                        name = ("A" if parity else "VOT", h)
                        w = MT if parity else NN
                        bank = unit(name)
                        for n, (a, b) in enumerate(((0, 0), (0, 1), (1, 0))):
                            i = pe.matmul(bank[:, 0:4 * KEYS], w[a][:, h, :], cT[b][:, :],
                                          start=(n == 0), stop=(n == 2))
                        done(i, name)

                def cross_scores(e):
                    wait(pe, s2_free, 2 * p + e)
                    for n in range(3):
                        a, b = n * 512, min((n + 1) * 512, HK)
                        i = pe.matmul(PS[:, n, 0:b - a], x1T[:, e, :], A[:, 2 * parity + e, a:b], start=True, stop=True)
                    i.then_inc(s2_full, 1)

                def cross_pT(e):
                    wait(pe, pn_done, 2 * p + e + 1)
                    for g, (a, b) in enumerate(GROUPS):
                        name = ("P2T", e, g)
                        bank = unit(name)
                        for c in range(a, b):
                            i = pe.transpose(bank[:, (c - a) * P:(c - a + 1) * P], pn[:, e, c * P:(c + 1) * P], ident[:, :])
                        done(i, name)

                def cross_out(e):
                    name = ("AV2", e)
                    bank = unit(name)
                    ring_wait_copied(pe, at, ("P2T", e, 2))
                    for c in range(CH):
                        i = pe.matmul(bank[:, 0:P], pT[:, e, c * P:(c + 1) * P], VO[parity][:, e, c, :],
                                      start=(c == 0), stop=(c == CH - 1))
                    done(i, name)

                def vo_transposes(pair, e):
                    for g, (a, b) in enumerate(GROUPS):
                        name = ("VO", pair, e, g)
                        bank = unit(name)
                        for c in range(a, b):
                            i = pe.transpose(bank[:, (c - a) * P:(c - a + 1) * P],
                                             VOT[:, 2 * pair + e, c * P:(c + 1) * P], ident[:, :])
                        done(i, name)

                def router():
                    bank = unit("LG")
                    ring_wait_copied(pe, at, "x2T")
                    for e in range(2):
                        i = pe.matmul(bank[:, e * E:(e + 1) * E], x2T[:, e, :], wr[:, :], start=True, stop=True)
                    done(i, "LG")

                def x_transposes():
                    wait(pe, x_in[parity], 16 * (nth + 2 - parity))
                    bank = unit("xT")
                    for e in range(2):
                        i = pe.transpose(bank[:, e * P:(e + 1) * P], xin[parity][:, e, :], ident[:, :])
                    done(i, "xT")

                def self_scores():
                    wait(pe, self_free, 3 * (p + 1))
                    ring_wait_copied(pe, at, "QK")
                    for e in range(2):
                        i = pe.matmul(small[:, e * P:(e + 1) * P], qT[:, e, :], kT[:, e, :], start=True, stop=True)
                    i.then_inc(self_full, 1)

                def self_transposes():
                    wait(pe, sexp_done, 2 * (p + 1) + 2)
                    for e in range(2):
                        i = pe.transpose(small[:, e * P:(e + 1) * P], pself[:, e, :], ident[:, :])
                    i.then_inc(self_full, 1)

                def self_values():
                    wait(pe, self_free, 3 * (p + 1) + 1)
                    for e in range(2):
                        i = pe.matmul(small[:, e * P:(e + 1) * P], pselfT[:, e, :], vs[:, e, :], start=True, stop=True)
                    i.then_inc(self_full, 1)

                first = prep and not cross
                alone = isinstance(p, int) and p == PAIRS - 1
                even, odd = ahead and parity == 0, prep and parity == 1
                products = even or odd
                if cross:
                    wait(pe, self_free, 3 * p + 3)
                    cross_scores(0)
                if parity == 0 and prep:
                    vo_transposes(1, 1)
                if even:
                    for k in range(2):
                        wait(pe, c_in[k], 16 * (nth + 2))
                    bank = unit("cT")
                    for b in range(4):
                        i = pe.transpose(bank[:, b * KEYS:(b + 1) * KEYS], cin[b // 2][:, b % 2, :], ident[0:KEYS, 0:KEYS])
                    done(i, "cT")
                    keep_warm(0 if cross else WARM["context"])
                if prep:
                    bank = unit("QK")
                    ring_wait_copied(pe, step_before(at), "xT")
                    for j in range(2):
                        i = pe.matmul(bank[:, j * 2 * P:(j + 1) * 2 * P], wT[:, j, :],
                                      xT[:, :, :].rearrange("p e t -> p (e t)"), start=True, stop=True)
                    done(i, "QK")
                    bank = unit("V")
                    for e in range(2):
                        i = pe.matmul(bank[:, e * P:(e + 1) * P], xT[:, e, :], wvo[:, 0, :], start=True, stop=True)
                    done(i, "V")
                if post:
                    wait(pe, x2_done, 2 * (p - 1) + 2)
                    bank = unit("x2T")
                    for e in range(2):
                        i = pe.transpose(bank[:, e * P:(e + 1) * P], x2[1 - parity][:, e, :], ident[:, :])
                    done(i, "x2T")
                if first:
                    self_scores()
                if odd:
                    vo_transposes(0, 0)
                    vo_transposes(0, 1)
                if first:
                    self_transposes()
                if cross:
                    keep_warm(14 if alone else 0)
                    cross_scores(1)
                if prep and cross:
                    self_scores()
                if even:
                    ring_wait_copied(pe, at, "cT")
                if products:
                    heads(0, 4)
                if first:
                    self_values()
                if post and parity == 1:
                    router()
                if products:
                    heads(4, 8)
                if products:
                    heads(8, 12)
                if prep and cross:
                    self_transposes()
                if cross:
                    keep_warm(6 if alone else 0)
                    cross_pT(0)
                if products:
                    heads(12, 14)
                if prep and cross:
                    self_values()
                if products:
                    heads(14, 16)
                if ahead and parity == 1:
                    x_transposes()
                if cross:
                    keep_warm(10 if alone else 0)
                    cross_out(0)
                    cross_pT(1)
                if post and parity == 0:
                    router()
                if even:
                    x_transposes()
                if odd:
                    vo_transposes(1, 0)
                if prep:
                    wait(pe, x1_done, 2 * (p + 1) + 2)
                    for e in range(2):
                        i = pe.transpose(small[:, e * P:(e + 1) * P], x1[1 - parity][:, e, :], ident[:, :])
                    i.then_inc(self_full, 1)
                if cross:
                    cross_out(1)

            attention_steps(pe, step)

            for k in range(RING_BANKS):
                n = sum(active(q, stage) for q in range(-2, PAIRS + 1) for j, (_, stage) in enumerate(UNITS[q % 2])
                        if j % RING_BANKS == k)
                pe.wait_ge(free[k], n)
            pe.wait_ge(consts, CONSTS)
            pe.transpose(PS[:, 4, 0:E * FC], b1n[:, :], ident[0:E * FC, 0:E * FC])
            pe.transpose(PS[:, 4, P:2 * P], groupf[:, :], ident[:, :]).then_inc(late_full, 1)
            pe.wait_ge(gates_done, 1)
            for g in range(2):
                i = pe.transpose(PS[:, 0, g * P:(g + 1) * P],
                                 gates[:, B // 2 * g:B // 2 * (g + 1), :].rearrange("p b e -> p (b e)"), ident[:, :])
            i.then_inc(gatesT_full, 1)
            pe.wait_ge(late_done, 2)
            for r in range(ROUNDS):
                pe.wait_ge(counted, r + 1)
                pe.matmul(PS[:, 1, 0:7], group[:, :], count[:, r % 2, :], start=True, stop=True).then_inc(summed, 1)
                if r < 2:
                    pe.matmul(PS[:, 5 + r, :], ones[0:1, :], brow[0:1, P + 512 * r:P + 512 * (r + 1)],
                              start=True, stop=True).then_inc(late_full, 1)
            pe.wait_ge(thr8_done, 1)
            pe.matmul(PS[:, 1, 8:8 + E], ones[0:E, :], thr8[:, :], start=True, stop=True).then_inc(thrb_full, 1)
            pe.wait_ge(taken_done, 1)
            t = taken[:, :, :, :].rearrange("p e a b -> p (e a b)")
            pe.matmul(PS[:, 2, :], before[:, :], t, start=True, stop=True)
            pe.matmul(PS[:, 3, :], onesb[:, :], t, start=True, stop=True).then_inc(prefix_full, 1)

            def make_list(e):
                pe.wait_ge(tokens_done, e + 1)
                if e:
                    pe.wait_ge(idx_done, e)
                for b in range(B):
                    if b % (B // 4) == 0:
                        pe.wait_ge(onehot_done, 4 * e + b // (B // 4) + 1)
                    i = pe.matmul(PS[:, 7, 0:2 * SB], onehot[:, b, :], tokens[:, b, :, :].rearrange("p s a -> p (s a)"),
                                  start=(b == 0), stop=(b == B - 1))
                i.then_inc(list_full, 1)

            def transpose_rows(e, h):
                if e:
                    pe.wait_ge(xeT_done, 2 * (e - 1) + h + 1)
                for s in range(4):
                    pe.wait_ge(gathered[e % 3][4 * h + s], 16 * (e // 3 + 1))
                    i = pe.transpose(PS[:, 3 + h, s * P:(s + 1) * P], xg[:, e % 3, 4 * h + s, 0:P], ident[:, :])
                i.then_inc(xeT_full, 1)

            def hidden(e, h):
                pe.wait_ge(xeT_done, 2 * e + h + 1)
                for c in range(FC):
                    k = 2 * FC * e + FC * h + c
                    if k >= 3:
                        pe.wait_ge(hid_done, k - 2)
                    pe.matmul(PS[:, HID_BANKS[k % 3], :], w1[:, e, c * P:(c + 1) * P], xeT[:, 512 * h:512 * h + 512],
                              start=True, stop=True).then_inc(hid_full, 1)

            def second_layer(e, h):
                if e < E - 1:
                    pe.wait_ge(hid_done, 2 * FC * e + FC * (h + 1))
                if e == E - 1:
                    pe.wait_ge(ye_added, 2 * e)
                elif e:
                    pe.wait_ge(ye_added, 2 * (e - 1) + h + 1)
                for s in range(4):
                    if e == E - 1 and h:
                        pe.wait_ge(ye_added, blocks_through(e, s))
                    if e == E - 1 and s == 2:
                        pe.wait_ge(xeT_done, 2 * (e + 1))
                    for c in range(FC):
                        if e == E - 1 and s == 0:
                            pe.wait_ge(hid_done, 2 * FC * e + FC * h + c + 1)
                        i = pe.matmul(y_bank(e, h, s), hid[:, c, (4 * h + s) * P:(4 * h + s + 1) * P],
                                      w2[:, e, c, :], start=(c == 0), stop=(c == FC - 1))
                    if e == E - 1:
                        i.then_inc(ye_full, 1)
                if e < E - 1:
                    i.then_inc(ye_full, 1)

            make_list(0)
            make_list(1)
            pe.wait_ge(late_done, 3)
            pe.wait_ge(w1_in, 16)
            pe.wait_ge(w2_in, 16)
            transpose_rows(0, 0)
            for e in range(E):
                hidden(e, 0)
                if e == 0:
                    transpose_rows(0, 1)
                    make_list(2)
                if e < E - 1:
                    hidden(e, 1)
                    second_layer(e, 0)
                else:
                    transpose_rows(e, 1)
                    second_layer(e, 0)
                    hidden(e, 1)
                if e + 1 < E:
                    transpose_rows(e + 1, 0)
                if e + 1 < E - 1:
                    transpose_rows(e + 1, 1)
                if e + 3 < E:
                    make_list(e + 3)
                second_layer(e, 1)


_INS = ["x", "ctx_1024", "L0_attn_Wq", "L0_attn_bq", "L0_attn_Wk", "L0_attn_bk", "L0_attn_Wv", "L0_attn_bv",
        "L0_attn_Wo", "L0_attn_bo", "L0_xattn_W_Q", "L0_xattn_W_K", "L0_xattn_W_V", "L0_xattn_W_O",
        "L0_ffn_Wr", "L0_ffn_W1", "L0_ffn_b1", "L0_ffn_W2", "L0_ffn_b2"]


def kernel(**inputs):
    import numpy as _np
    import concourse.bacc as _bacc
    from concourse import mybir as _mybir
    from concourse.bass_utils import run_bass_kernel_spmd as _run

    nc = _bacc.Bacc("TRN2", target_bir_lowering=False, num_devices=1)
    arrays, args = {}, []
    for name in _INS:
        a = _np.ascontiguousarray(inputs[name])
        arrays[f"in_{name}"] = a
        args.append(nc.dram_tensor(f"in_{name}", a.shape, _mybir.dt.from_np(a.dtype), kind="ExternalInput").ap())
    args.append(nc.dram_tensor("out_x", (B, P, P), F32, kind="ExternalOutput").ap())
    decoder_layer(nc, *args)
    r = _run(nc, [arrays], core_ids=[0])
    return r.results[0]["out_x"]
```
